# Optimizing a Trainium2 kernel written in Bass

```python
import numpy as np
import jax
import jax.numpy as jnp

def _softmax(x, axis=-1):
    return jax.nn.softmax(x, axis=axis)

def _gelu(x):
    return jax.nn.gelu(x, approximate=True)

def _silu(x):
    return jax.nn.silu(x)

def _sigmoid(x):
    return jax.nn.sigmoid(x)

def _layernorm(x, axis=-1, eps=1e-05):
    m = jnp.mean(x, axis=axis, keepdims=True)
    v = jnp.var(x, axis=axis, keepdims=True)
    return (x - m) / jnp.sqrt(v + eps)

def _scatter_add(tgt, idx, src, axis=0):
    return tgt.at[idx].add(src)

def _segment_sum(src, seg, n):
    return jax.ops.segment_sum(src, seg, n)
kernel_name = 'mk_hybrid_d1_jaxref_r4_f2905c'

def setup_inputs(seed: int=0):
    np.random.seed(seed)
    _w = jnp.asarray

    def _L0_attn_a_setup():
        import jax, jax.numpy as jnp
        import numpy as np
        DIM = 256
        EPS = 1e-12

        def _rmsnorm(x, gamma):
            norm = jnp.sqrt(jnp.sum(x * x, axis=-1, keepdims=True))
            scale = jnp.asarray(np.sqrt(x.shape[-1]), x.dtype)
            return x / jnp.maximum(norm, EPS) * scale * gamma
        key = jax.random.key(seed)
        k1, k2, k3 = jax.random.split(key, 3)
        b, n, d = (2, 1024, DIM)
        x = jax.random.normal(k1, (b, n, d), dtype=jnp.float32)
        w_qkva = jax.random.normal(k2, (3 * d, d), dtype=jnp.float32) * (1.0 / np.sqrt(d))
        gamma = jnp.ones((d,), dtype=jnp.float32)
        return {'x': x, 'gamma': gamma, 'w_qkva': w_qkva}
    _L0_attn_a_in = _L0_attn_a_setup()

    def _L0_attn_b_setup():
        import jax, jax.numpy as jnp
        import numpy as np
        B, T, D = (2, 512, 256)
        H, DK, DV = (16, 64, 64)

        def _hla(x, W_q, W_k, W_v, W_o):
            b, t, _ = x.shape
            q = (x @ W_q).reshape(b, t, H, DK).transpose(1, 0, 2, 3)
            k = (x @ W_k).reshape(b, t, H, DK).transpose(1, 0, 2, 3)
            v = (x @ W_v).reshape(b, t, H, DV).transpose(1, 0, 2, 3)
            S_K0 = jnp.zeros((b, H, DK, DK), x.dtype)
            C_QV0 = jnp.zeros((b, H, DK, DV), x.dtype)
            G0 = jnp.zeros((b, H, DK, DV), x.dtype)

            def step(carry, qkv):
                S_K, C_QV, G = carry
                q_t, k_t, v_t = qkv
                k_C = jnp.einsum('bhk,bhkv->bhv', k_t, C_QV)
                G = G + k_t[..., :, None] * k_C[..., None, :]
                S_K = S_K + k_t[..., :, None] * k_t[..., None, :]
                C_QV = C_QV + q_t[..., :, None] * v_t[..., None, :]
                S_C = jnp.einsum('bhkj,bhjv->bhkv', S_K, C_QV)
                o_t = jnp.einsum('bhk,bhkv->bhv', q_t, S_C - G)
                return ((S_K, C_QV, G), o_t)
            _, outs = jax.lax.scan(step, (S_K0, C_QV0, G0), (q, k, v))
            out = outs.transpose(1, 0, 2, 3).reshape(b, t, H * DV)
            return out @ W_o
        key = jax.random.key(seed)
        ks = jax.random.split(key, 5)
        scale = 0.1 * (6.0 / (D + D)) ** 0.5
        return {'x': jax.random.normal(ks[0], (B, T, D), dtype=jnp.float32), 'W_q': jax.random.normal(ks[1], (D, H * DK), dtype=jnp.float32) * scale, 'W_k': jax.random.normal(ks[2], (D, H * DK), dtype=jnp.float32) * scale, 'W_v': jax.random.normal(ks[3], (D, H * DV), dtype=jnp.float32) * scale, 'W_o': jax.random.normal(ks[4], (H * DV, D), dtype=jnp.float32) * scale}
    _L0_attn_b_in = _L0_attn_b_setup()

    def _L0_ffn_setup():
        import jax, jax.numpy as jnp
        import numpy as np
        EMB = 256
        FF = 4 * EMB

        def _ternary(w):
            scale = jnp.maximum(jnp.mean(jnp.abs(w)), 1e-08)
            w_t = jnp.clip(jnp.round(w / scale), -1.0, 1.0)
            return w + jax.lax.stop_gradient(w_t - w)
        key = jax.random.key(seed)
        kx, k1, k2, kb1, kb2 = jax.random.split(key, 5)
        x = jax.random.normal(kx, (4, 512, EMB), dtype=jnp.float32)
        lim1 = 1.0 / np.sqrt(EMB)
        lim2 = 1.0 / np.sqrt(FF)
        W1 = jax.random.uniform(k1, (FF, EMB), jnp.float32, -lim1, lim1)
        b1 = jax.random.uniform(kb1, (FF,), jnp.float32, -lim1, lim1)
        W2 = jax.random.uniform(k2, (EMB, FF), jnp.float32, -lim2, lim2)
        b2 = jax.random.uniform(kb2, (EMB,), jnp.float32, -lim2, lim2)
        return {'x': x, 'W1': W1, 'b1': b1, 'W2': W2, 'b2': b2}
    _L0_ffn_in = _L0_ffn_setup()
    _d = {'L0_attn_a_x': _L0_attn_a_in['x'], 'L0_attn_a_gamma': _L0_attn_a_in['gamma'], 'L0_attn_a_w_qkva': _L0_attn_a_in['w_qkva'], 'L0_attn_b_W_q': _L0_attn_b_in['W_q'], 'L0_attn_b_W_k': _L0_attn_b_in['W_k'], 'L0_attn_b_W_v': _L0_attn_b_in['W_v'], 'L0_attn_b_W_o': _L0_attn_b_in['W_o'], 'L0_ffn_W1': _L0_ffn_in['W1'], 'L0_ffn_b1': _L0_ffn_in['b1'], 'L0_ffn_W2': _L0_ffn_in['W2'], 'L0_ffn_b2': _L0_ffn_in['b2']}
    _x0 = _d['L0_attn_a_x']
    _d['L0_attn_a_x'] = jax.random.normal(jax.random.fold_in(jax.random.key(seed), 1), (2, 2048, 256), dtype=_x0.dtype)
    del _x0
    return _d

def reference(L0_attn_a_x, L0_attn_a_gamma, L0_attn_a_w_qkva, L0_attn_b_W_q, L0_attn_b_W_k, L0_attn_b_W_v, L0_attn_b_W_o, L0_ffn_W1, L0_ffn_b1, L0_ffn_W2, L0_ffn_b2):

    def _L0_attn_a_ref(x, gamma, w_qkva):
        import jax, jax.numpy as jnp
        import numpy as np
        DIM = 256
        EPS = 1e-12

        def _rmsnorm(x, gamma):
            norm = jnp.sqrt(jnp.sum(x * x, axis=-1, keepdims=True))
            scale = jnp.asarray(np.sqrt(x.shape[-1]), x.dtype)
            return x / jnp.maximum(norm, EPS) * scale * gamma
        d = x.shape[-1]
        xn = _rmsnorm(x, gamma)
        qkva = jnp.einsum('bnd,ed->bne', xn, w_qkva)
        q, kv, a = (qkva[..., :d], qkva[..., d:2 * d], qkva[..., 2 * d:])
        a = jax.nn.sigmoid(a)

        def binary_operator(e_i, e_j):
            a_i, kv_i = e_i
            a_j, kv_j = e_j
            return (a_j * a_i, a_j * kv_i + kv_j)
        _, kv_scan = jax.lax.associative_scan(binary_operator, (a, kv), axis=1)
        return q * kv_scan

    def _L0_attn_b_ref(x, W_q, W_k, W_v, W_o):
        import jax, jax.numpy as jnp
        import numpy as np
        B, T, D = (2, 512, 256)
        H, DK, DV = (16, 64, 64)

        def _hla(x, W_q, W_k, W_v, W_o):
            b, t, _ = x.shape
            q = (x @ W_q).reshape(b, t, H, DK).transpose(1, 0, 2, 3)
            k = (x @ W_k).reshape(b, t, H, DK).transpose(1, 0, 2, 3)
            v = (x @ W_v).reshape(b, t, H, DV).transpose(1, 0, 2, 3)
            S_K0 = jnp.zeros((b, H, DK, DK), x.dtype)
            C_QV0 = jnp.zeros((b, H, DK, DV), x.dtype)
            G0 = jnp.zeros((b, H, DK, DV), x.dtype)

            def step(carry, qkv):
                S_K, C_QV, G = carry
                q_t, k_t, v_t = qkv
                k_C = jnp.einsum('bhk,bhkv->bhv', k_t, C_QV)
                G = G + k_t[..., :, None] * k_C[..., None, :]
                S_K = S_K + k_t[..., :, None] * k_t[..., None, :]
                C_QV = C_QV + q_t[..., :, None] * v_t[..., None, :]
                S_C = jnp.einsum('bhkj,bhjv->bhkv', S_K, C_QV)
                o_t = jnp.einsum('bhk,bhkv->bhv', q_t, S_C - G)
                return ((S_K, C_QV, G), o_t)
            _, outs = jax.lax.scan(step, (S_K0, C_QV0, G0), (q, k, v))
            out = outs.transpose(1, 0, 2, 3).reshape(b, t, H * DV)
            return out @ W_o
        return _hla(x, W_q, W_k, W_v, W_o)

    def _L0_ffn_ref(x, W1, b1, W2, b2):
        import jax, jax.numpy as jnp
        import numpy as np
        EMB = 256
        FF = 4 * EMB

        def _ternary(w):
            scale = jnp.maximum(jnp.mean(jnp.abs(w)), 1e-08)
            w_t = jnp.clip(jnp.round(w / scale), -1.0, 1.0)
            return w + jax.lax.stop_gradient(w_t - w)
        h = jnp.einsum('bsd,fd->bsf', x, _ternary(W1)) + b1
        h = jax.nn.gelu(h, approximate=False)
        out = jnp.einsum('bsf,df->bsd', h, _ternary(W2)) + b2
        return out
    x = L0_attn_a_x
    x = x + _L0_attn_a_ref(_layernorm(x, axis=-1), L0_attn_a_gamma, L0_attn_a_w_qkva)
    x = x + _L0_ffn_ref(_layernorm(x, axis=-1), L0_ffn_W1, L0_ffn_b1, L0_ffn_W2, L0_ffn_b2)
    x = x + _L0_attn_b_ref(_layernorm(x, axis=-1), L0_attn_b_W_q, L0_attn_b_W_k, L0_attn_b_W_v, L0_attn_b_W_o)
    x = x + _L0_ffn_ref(_layernorm(x, axis=-1), L0_ffn_W1, L0_ffn_b1, L0_ffn_W2, L0_ffn_b2)
    return x

_drawn_inputs = setup_inputs


def setup_inputs(seed=0):
    import zlib

    import numpy as np

    out = dict(_drawn_inputs(seed))
    spreads = {'L0_attn_a_gamma': (1.0, 0.2)}
    factors = {'L0_ffn_b1': 8.0, 'L0_ffn_b2': 200.0}
    for name, (base, spread) in spreads.items():
        noise = np.random.default_rng([zlib.crc32(name.encode()), seed]).standard_normal(out[name].shape)
        drawn = base * np.exp(spread * noise) if base else spread * noise
        out[name] = jnp.asarray(drawn.astype(out[name].dtype))
    for name, factor in factors.items():
        out[name] = (out[name] * factor).astype(out[name].dtype)
    return out
```

```python
import concourse.bass as bass
from concourse import mybir
from contextlib import ExitStack

FP32 = mybir.dt.float32
FP32R = mybir.dt.float32r
ALU = mybir.AluOpType
ACT = mybir.ActivationFunctionType
AX = mybir.AxisListType

START = 1

P = 128
B, T, D = 2, 2048, 256
DC = D // P
BLK = 512
CH = BLK // P
NBLK = T // BLK
TILES = T // P
FF = 1024
FC = FF // P
H, DK = 16, 64
PAIRS = H // 2
QKVA = 3 * D
LN_EPS = 1e-5
RMS_EPS = 1e-12


def hybrid_kernel(nc, x_d, gamma_d, wqkva_d, wq_d, wk_d, wv_d, wo_d, w1_d, b1_d, w2_d, b2_d, out_d):
    x_view = x_d.rearrange("b (n p) d -> b p n d", p=P)
    out_view = out_d.rearrange("b (n p) d -> b p n d", p=P)
    wq_view = wq_d.rearrange("(k p) (n c) -> p n k c", p=P, c=P)
    wk_view = wk_d.rearrange("(k p) (n c) -> p n k c", p=P, c=P)

    outer = ExitStack()
    with outer:
        def sbuf(stack, name, shape, dtype=FP32):
            return stack.enter_context(nc.sbuf_tensor(name, shape, dtype))

        def semaphores(stack):
            used = []

            @stack.callback
            def _():
                with nc.Block() as block:
                    @block.gpsimd
                    def _(pool):
                        nums = sorted(s.num for s in used)
                        starts = [n for n in nums if n - 1 not in nums]
                        ends = [n + 1 for n in nums if n + 1 not in nums]
                        for first, end in zip(starts, ends):
                            pool.sem_clear(range(first, end))
                for s in used:
                    nc.release_semaphore(s)

            def sem(name):
                used.append(nc.alloc_semaphore(name))
                return used[-1]

            def sems(name):
                return [sem(f"{name}{b}") for b in range(B)]
            return sem, sems

        xres = sbuf(outer, "xres", [P, B * TILES * D])
        ident = sbuf(outer, "ident", [P, P])
        wv_hi = sbuf(outer, "wv_hi", [P, DC, H * DK], FP32R)
        wv_lo = sbuf(outer, "wv_lo", [P, DC, H * DK], FP32R)
        wo_hi = sbuf(outer, "wo_hi", [P, PAIRS * D], FP32R)
        wo_lo = sbuf(outer, "wo_lo", [P, PAIRS * D], FP32R)
        b1_sb = sbuf(outer, "b1_sb", [P, FC])
        b2_sb = sbuf(outer, "b2_sb", [P, D])
        gamma_sb = sbuf(outer, "gamma_sb", [P, DC])
        ln_stats = sbuf(outer, "ln_stats", [P, B, CH, 6])
        ln_moments = sbuf(outer, "ln_moments", [P, B, CH, 2])
        ln_vare = sbuf(outer, "ln_vare", [P, B, CH])
        ln_rstd = sbuf(outer, "ln_rstd", [P, B, CH])
        ln_filler = sbuf(outer, "ln_filler", [P, 1])
        ln_eps = sbuf(outer, "ln_eps", [P, CH])
        minus_half = sbuf(outer, "minus_half", [P, CH])
        plus_half = sbuf(outer, "plus_half", [P, CH])
        bank = [outer.enter_context(nc.psum_tensor(f"bank{i}", [P, BLK], FP32)) for i in range(8)]
        w1t_dram = nc.dram_tensor("w1t_scratch", (P, DC * FF), FP32, kind="Internal").ap()
        w2t_dram = nc.dram_tensor("w2t_scratch", (P, FC * D), FP32, kind="Internal").ap()

        def start_counts(eng, *semaphores_of_eng):
            for s in semaphores_of_eng:
                for one in (s if isinstance(s, list) else [s]):
                    eng.sem_inc(one, START)

        def rows(b, i, c=0, n=1):
            return xres[:, bass.ds((i * CH + (b * TILES + c)) * D, n * D)]

        class LayerNorm:
            def __init__(self, stack, sems, tag):
                self.xn = sbuf(stack, f"{tag}_xn", [P, B, CH, D])
                self.xhi = sbuf(stack, f"{tag}_xhi", [P, B, DC, BLK], FP32R)
                self.xlo = sbuf(stack, f"{tag}_xlo", [P, B, DC, BLK], FP32R)
                self.stats_done = sems(f"{tag}_stats")
                self.moments_done = sems(f"{tag}_moments")
                self.rstd_done = sems(f"{tag}_rstd")
                self.vare_done = sems(f"{tag}_vare")
                self.normalised = sems(f"{tag}_normal")
                self.transposed = sems(f"{tag}_transp")
                self.high_done = sems(f"{tag}_xhigh")
                self.low_done = sems(f"{tag}_xlow")

            def dve_statistics(self, dve, b, i):
                for c in range(CH):
                    nc.vector.bn_stats(ln_stats[:, b, c, :], rows(b, i, c)).then_inc(self.stats_done[b], 1)
                dve.wait_ge(self.stats_done[b], START + (i + 1) * CH)
                nc.vector.memset(ln_filler[:, :], 0.0)
                for c in range(CH):
                    nc.vector.bn_aggr(ln_moments[:, b, c, :], ln_stats[:, b, c, :]).then_inc(self.moments_done[b], 1)

            def pool_rstd(self, pool, b, i):
                pool.wait_ge(self.moments_done[b], START + (i + 1) * CH)
                nc.gpsimd.tensor_tensor(ln_vare[:, b, :], ln_moments[:, b, :, 1], ln_eps[:, :],
                                        ALU.add).then_inc(self.vare_done[b], 1)
                pool.wait_ge(self.vare_done[b], START + i + 1)
                nc.gpsimd.tensor_tensor(ln_rstd[:, b, :], ln_vare[:, b, :], minus_half[:, :],
                                        ALU.pow).then_inc(self.rstd_done[b], 1)

            def dve_normalise(self, dve, b, i, factor=None):
                dve.wait_ge(self.transposed[b], START + i * DC)
                for c in range(CH):
                    scale = (ln_rstd if factor is None else factor)[:, b, c:c + 1]
                    nc.vector.tensor_scalar(self.xn[:, b, c, :], rows(b, i, c), ln_moments[:, b, c, 0:1],
                                            scale, ALU.subtract, ALU.mult).then_inc(self.normalised[b], 1)

            def pe_transpose(self, pe, b, i, banks):
                pe.wait_ge(self.normalised[b], START + (i + 1) * CH)
                for k in range(DC):
                    for c in range(CH):
                        last = nc.tensor.transpose(bank[banks[k]][:, c * P:(c + 1) * P],
                                                   self.xn[:, b, c, k * P:(k + 1) * P], ident[:, :])
                    last.then_inc(self.transposed[b], 1)

            def act_high(self, act, b, i, banks, scale=None):
                for k in range(DC):
                    act.wait_ge(self.transposed[b], START + i * DC + k + 1)
                    nc.scalar.activation(self.xhi[:, b, k, :], bank[banks[k]][:, :], ACT.Identity,
                                         scale=1.0 if scale is None else scale[:, k:k + 1])\
                        .then_inc(self.high_done[b], 1)

            def dve_low(self, dve, b, i, banks, scale=None):
                for k in range(DC):
                    dve.wait_ge(self.high_done[b], START + i * DC + k + 1)
                    if scale is None:
                        nc.vector.tensor_tensor(self.xlo[:, b, k, :], bank[banks[k]][:, :],
                                                self.xhi[:, b, k, :].bitcast(FP32), ALU.subtract)\
                            .then_inc(self.low_done[b], 1)
                    else:
                        nc.vector.scalar_tensor_tensor(self.xlo[:, b, k, :], bank[banks[k]][:, :],
                                                       scale[:, k:k + 1], self.xhi[:, b, k, :].bitcast(FP32),
                                                       ALU.mult, ALU.subtract).then_inc(self.low_done[b], 1)

        def pe_split_product(out, w_hi, w_lo, x_hi, x_lo, k, last_k):
            nc.tensor.matmul(out, w_hi, x_hi, start=(k == 0), stop=False)
            nc.tensor.matmul(out, w_hi, x_lo, start=False, stop=False)
            return nc.tensor.matmul(out, w_lo, x_hi, start=False, stop=(k == last_k))

        tern = outer.enter_context(ExitStack())
        w1t = sbuf(tern, "w1t", [P, DC, FF], FP32R)
        w2t = sbuf(tern, "w2t", [P, FC, D], FP32R)
        wqa = tern.enter_context(ExitStack())
        wa_hi = sbuf(wqa, "wa_hi", [P, DC, QKVA], FP32R)
        wa_lo = sbuf(wqa, "wa_lo", [P, DC, QKVA], FP32R)

        with ExitStack() as st:
            sem, _ = semaphores(st)
            wa_nat = sbuf(st, "wa_nat", [P, QKVA // P, D])
            w1_nat = sbuf(st, "w1_nat", [P, FC, D])
            w2_nat = sbuf(st, "w2_nat", [P, DC, FF])
            w1_neg = sbuf(st, "w1_neg", [P, FC, D])
            w2_neg = sbuf(st, "w2_neg", [P, DC, FF])
            wv_raw = sbuf(st, "wv_raw", [P, DC, H * DK])
            wo_raw = sbuf(st, "wo_raw", [P, PAIRS * D])
            ones = sbuf(st, "ones", [P, P])
            abs_sum = sbuf(st, "abs_sum", [P, 2])
            thr = sbuf(st, "thr", [P, 2])
            nthr = sbuf(st, "nthr", [P, 2])
            x_loaded = sem("x_loaded")
            wa_loaded, w12_loaded, wvo_loaded, small_loaded = sem("wa_loaded"), sem("w12_loaded"), sem("wvo_loaded"), sem("small_loaded")
            ident_zero, ident_done, ones_done = sem("ident_zero"), sem("ident_done"), sem("ones_done")
            abs_done, sum_done, thr_step, tern_neg, tern_done = sem("abs_done"), sem("sum_done"), sem("thr_step"), sem("tern_neg"), sem("tern_done")
            wa_t, wa_h, wa_l = sem("wa_t"), sem("wa_h"), sem("wa_l")
            w_t, w_evac, w_saved = sem("w_t"), sem("w_evac"), sem("w_saved")
            wvo_high, wvo_low = sem("wvo_high"), sem("wvo_low")
            block = st.enter_context(nc.Block())

            @block.sync
            def _(sp):
                for n in range(NBLK):
                    for b in range(B):
                        sp.dma_start(rows(b, n, 0, CH).rearrange("p (n d) -> p n d", d=D),
                                     x_view[b, :, n * CH:(n + 1) * CH, :]).then_inc(x_loaded, 16)
                sp.wait_ge(w_evac, 8)
                sp.dma_start(w1t_dram, w1t[:, :, :].rearrange("p a b -> p (a b)").bitcast(FP32)).then_inc(w_saved, 16)
                sp.dma_start(w2t_dram, w2t[:, :, :].rearrange("p a b -> p (a b)").bitcast(FP32)).then_inc(w_saved, 16)
                sp.wait_ge(w_saved, 32)
                sp.wait_ge(x_loaded, 16 * NBLK * B)

            @block.gpsimd
            def _(pool):
                nc.gpsimd.memset(ident[:, :], 0.0).then_inc(ident_zero, 1)
                nc.gpsimd.memset(ones[:, :], 1.0).then_inc(ones_done, 1)
                nc.gpsimd.memset(minus_half[:, :], -0.5)
                nc.gpsimd.memset(plus_half[:, :], 0.5)
                nc.gpsimd.memset(ln_eps[:, :], LN_EPS)
                pool.wait_ge(ident_zero, 1)
                nc.gpsimd.affine_select(out=ident[:, :], in_=ident[:, :], compare_op=ALU.not_equal, fill=1.0,
                                        base=0, pattern=[[-1, P]], channel_multiplier=1).then_inc(ident_done, 1)

            @block.scalar
            def _(act):
                act.dma_start(wa_nat[:, :, :], wqkva_d.rearrange("(n p) d -> p n d", p=P)).then_inc(wa_loaded, 16)
                act.dma_start(w1_nat[:, :, :], w1_d.rearrange("(n p) d -> p n d", p=P)).then_inc(w12_loaded, 16)
                act.dma_start(w2_nat[:, :, :], w2_d.rearrange("(n p) d -> p n d", p=P)).then_inc(w12_loaded, 16)
                act.dma_start(wv_raw[:, :, :], wv_d.rearrange("(k p) c -> p k c", p=P)).then_inc(wvo_loaded, 16)
                act.dma_start(wo_raw[:, :].rearrange("p (n d) -> p n d", d=D),
                              wo_d.rearrange("(n p) d -> p n d", p=P)).then_inc(wvo_loaded, 16)
                act.dma_start(b1_sb[:, :], b1_d.rearrange("(n p) -> p n", p=P), allow_slow_non_contiguous=True).then_inc(small_loaded, 16)
                act.dma_start(gamma_sb[:, :], gamma_d.rearrange("(n p) -> p n", p=P), allow_slow_non_contiguous=True).then_inc(small_loaded, 16)
                act.dma_start(b2_sb[:, :], b2_d.partition_broadcast(P)).then_inc(small_loaded, 16)
                for n in range(3):
                    act.wait_ge(wa_t, n + 1)
                    nc.scalar.copy(wa_hi[:, :, :].rearrange("p a b -> p (a b)")[:, n * BLK:(n + 1) * BLK],
                                   bank[n][:, :]).then_inc(wa_h, 1)
                for n in range(8):
                    act.wait_ge(w_t, n + 1)
                    dst = (w1t if n < 4 else w2t)[:, :, :].rearrange("p a b -> p (a b)")
                    nc.scalar.copy(dst[:, (n % 4) * BLK:(n % 4 + 1) * BLK], bank[3 + n % 4][:, :]).then_inc(w_evac, 1)
                act.wait_ge(small_loaded, 48)

            @block.tensor
            def _(pe):
                pe.wait_ge(wa_loaded, 16)
                pe.wait_ge(ident_done, 1)
                for m in range(DC * QKVA // P):
                    k, r = m // (QKVA // P), m % (QKVA // P)
                    last = nc.tensor.transpose(bank[m // 4][:, (m % 4) * P:(m % 4 + 1) * P],
                                               wa_nat[:, r, k * P:(k + 1) * P], ident[:, :])
                    if m % 4 == 3:
                        last.then_inc(wa_t, 1)
                pe.wait_ge(abs_done, 2)
                pe.wait_ge(ones_done, 1)
                nc.tensor.matmul(bank[7][:, 0:2], ones[:, :], abs_sum[:, :], start=True, stop=True).then_inc(sum_done, 1)
                for n in range(8):
                    pe.wait_ge(tern_done, 1 if n < 4 else 2)
                    if n >= 4:
                        pe.wait_ge(w_evac, n - 3)
                    for m in range(4):
                        if n < 4:
                            src = w1_nat[:, (n % 2) * 4 + m, (n // 2) * P:(n // 2 + 1) * P]
                        else:
                            f = 2 * (n - 4) + m // 2
                            src = w2_nat[:, m % 2, f * P:(f + 1) * P]
                        last = nc.tensor.transpose(bank[3 + n % 4][:, m * P:(m + 1) * P], src, ident[:, :])
                    last.then_inc(w_t, 1)

            @block.vector
            def _(dve):
                for n in range(3):
                    dve.wait_ge(wa_h, n + 1)
                    nc.vector.tensor_tensor(wa_lo[:, :, :].rearrange("p a b -> p (a b)")[:, n * BLK:(n + 1) * BLK],
                                            bank[n][:, :],
                                            wa_hi[:, :, :].rearrange("p a b -> p (a b)")[:, n * BLK:(n + 1) * BLK].bitcast(FP32),
                                            ALU.subtract).then_inc(wa_l, 1)
                dve.wait_ge(w12_loaded, 32)
                nc.vector.tensor_reduce(abs_sum[:, 0:1], w1_nat[:, :, :], AX.XY, ALU.add, apply_absolute_value=True).then_inc(abs_done, 1)
                nc.vector.tensor_reduce(abs_sum[:, 1:2], w2_nat[:, :, :], AX.XY, ALU.add, apply_absolute_value=True).then_inc(abs_done, 1)
                dve.wait_ge(sum_done, 1)
                nc.vector.tensor_scalar(thr[:, :], bank[7][:, 0:2], 1.0 / (FF * D), 1e-8, ALU.mult, ALU.max).then_inc(thr_step, 1)
                dve.wait_ge(thr_step, 1)
                nc.vector.tensor_scalar(nthr[:, :], thr[:, :], -0.5, None, ALU.mult).then_inc(thr_step, 1)
                dve.wait_ge(thr_step, 2)
                nc.vector.tensor_scalar(thr[:, :], thr[:, :], 0.5, None, ALU.mult).then_inc(thr_step, 1)
                dve.wait_ge(thr_step, 3)
                for n, (nat, neg) in enumerate(((w1_nat, w1_neg), (w2_nat, w2_neg))):
                    nc.vector.tensor_scalar(neg[:, :, :], nat[:, :, :], nthr[:, n:n + 1], None, ALU.is_lt).then_inc(tern_neg, 1)
                    dve.wait_ge(tern_neg, n + 1)
                    nc.vector.scalar_tensor_tensor(nat[:, :, :], nat[:, :, :], thr[:, n:n + 1], neg[:, :, :],
                                                   ALU.is_gt, ALU.subtract).then_inc(tern_done, 1)
                dve.wait_ge(wvo_loaded, 32)
                for n, (raw, hi, lo) in enumerate(((wv_raw[:, :, :], wv_hi[:, :, :], wv_lo[:, :, :]),
                                                   (wo_raw[:, :], wo_hi[:, :], wo_lo[:, :]))):
                    nc.vector.tensor_copy(hi, raw).then_inc(wvo_high, 1)
                    dve.wait_ge(wvo_high, n + 1)
                    nc.vector.tensor_tensor(lo, raw, hi.bitcast(FP32), ALU.subtract).then_inc(wvo_low, 1)

        with ExitStack() as st:
            sem, sems = semaphores(st)
            ln = LayerNorm(st, sems, "A")
            rms_std = sbuf(st, "rms_std", [P, B, CH])
            rms_norm = sbuf(st, "rms_norm", [P, B, CH])
            rms_factor = sbuf(st, "rms_factor", [P, B, CH])
            gate = sbuf(st, "gate", [P, B, DC, BLK])
            scan = sbuf(st, "scan", [P, B, DC, BLK])
            carry = sbuf(st, "carry", [P, B * DC])
            y = sbuf(st, "y", [P, B, DC, BLK])
            std_done, rms_step, factor_done = sems("A_std"), sems("A_rmsstep"), sems("A_factor")
            kv_ready, a_ready, q_ready = sems("A_kv"), sems("A_a"), sems("A_q")
            gate_done, scan_done, carry_done, y_done = sems("A_gate"), sems("A_scan"), sems("A_carry"), sems("A_y")
            y_transposed, x_added, carry_zero = sems("A_yt"), sems("A_xadd"), sem("A_zero")
            XB, KV, AB, QB, YB = (0, 1), (2, 3), 4, 5, (6, 7)
            block = st.enter_context(nc.Block())

            def a_prepare_dve(dve, b, i):
                dve.wait_ge(rms_step[b], START + 3 * i)
                ln.dve_statistics(dve, b, i)

            def a_factor_dve(dve, b, i):
                dve.wait_ge(std_done[b], START + i + 1)
                nc.vector.scalar_tensor_tensor(rms_norm[:, b, :], ln_rstd[:, b, :], float(D) ** 0.5, rms_std[:, b, :],
                                               ALU.mult, ALU.mult).then_inc(rms_step[b], 1)
                dve.wait_ge(rms_step[b], START + 3 * i + 1)
                nc.vector.tensor_scalar(rms_norm[:, b, :], rms_norm[:, b, :], RMS_EPS, None, ALU.max).then_inc(rms_step[b], 1)
                dve.wait_ge(rms_step[b], START + 3 * i + 2)
                nc.vector.reciprocal(rms_norm[:, b, :], rms_norm[:, b, :]).then_inc(rms_step[b], 1)
                dve.wait_ge(rms_step[b], START + 3 * i + 3)
                nc.vector.scalar_tensor_tensor(rms_factor[:, b, :], ln_rstd[:, b, :], float(D) ** 0.5, rms_norm[:, b, :],
                                               ALU.mult, ALU.mult).then_inc(factor_done[b], 1)
                dve.wait_ge(factor_done[b], START + i + 1)
                ln.dve_normalise(dve, b, i, factor=rms_factor)

            @block.gpsimd
            def _(pool):
                start_counts(pool, ln.vare_done, ln.rstd_done, std_done)
                def prepare(i):
                    for b in range(B):
                        ln.pool_rstd(pool, b, i)
                        nc.gpsimd.tensor_tensor(rms_std[:, b, :], ln_moments[:, b, :, 1], plus_half[:, :],
                                                ALU.pow).then_inc(std_done[b], 1)
                prepare(0)
                with pool.Fori(0, NBLK - 1) as i:
                    prepare(i + 1)

            @block.tensor
            def _(pe):
                start_counts(pe, ln.transposed, kv_ready, a_ready, q_ready, y_transposed)
                def project(b, i):
                    pe.wait_ge(ln.low_done[b], START + (i + 1) * DC)
                    x = [(ln.xhi[:, b, k, :], ln.xlo[:, b, k, :]) for k in range(DC)]
                    other = 1 - b
                    for h in range(DC):
                        for what, dst, part, ready in (("kv", KV[h], 1, kv_ready), ("a", AB, 2, a_ready), ("q", QB, 0, q_ready)):
                            if what == "kv":
                                if b:
                                    pe.wait_ge(scan_done[other], START + i * DC + h + 1)
                                else:
                                    pe.wait_ge(scan_done[other], START + i * DC)
                            elif what == "a":
                                if h:
                                    pe.wait_ge(gate_done[b], START + i * DC + 1)
                                else:
                                    pe.wait_ge(gate_done[other], START + (i + b) * DC)
                            else:
                                if h:
                                    pe.wait_ge(y_done[b], START + i * DC + 1)
                                else:
                                    pe.wait_ge(y_done[other], START + (i + b) * DC)
                            for k in range(DC):
                                cols = slice(part * D + h * P, part * D + (h + 1) * P)
                                last = pe_split_product(bank[dst][:, :], wa_hi[:, k, cols], wa_lo[:, k, cols],
                                                        x[k][0], x[k][1], k, DC - 1)
                            last.then_inc(ready[b], 1)

                def transpose_y(b, i):
                    for h in range(DC):
                        pe.wait_ge(y_done[b], START + i * DC + h + 1)
                        if h == 0:
                            pe.wait_ge(x_added[1 - b], START + (i + b) * 2)
                        for c in range(CH):
                            last = nc.tensor.transpose(bank[YB[c // 2]][:, (c % 2) * D + h * P:(c % 2) * D + (h + 1) * P],
                                                       y[:, b, h, c * P:(c + 1) * P], ident[:, :])
                    last.then_inc(y_transposed[b], 1)

                def prepare(b, i):
                    if b:
                        pe.wait_ge(ln.low_done[0], START + (i + 1) * DC)
                    else:
                        pe.wait_ge(ln.low_done[1], START + i * DC)
                    ln.pe_transpose(pe, b, i, XB)

                def body(i, more):
                    for b in range(B):
                        project(b, i)
                    if more:
                        for b in range(B):
                            prepare(b, i + 1)
                    for b in range(B):
                        transpose_y(b, i)

                for b in range(B):
                    prepare(b, 0)
                with pe.Fori(0, NBLK - 1) as i:
                    body(i, True)
                body(NBLK - 1, False)

            @block.scalar
            def _(act):
                start_counts(act, ln.high_done, gate_done)
                def body(i, more):
                    for b in range(B):
                        for h in range(DC):
                            act.wait_ge(a_ready[b], START + i * DC + h + 1)
                            act.wait_ge(scan_done[b], START + i * DC)
                            nc.scalar.activation(gate[:, b, h, :], bank[AB][:, :], ACT.Sigmoid).then_inc(gate_done[b], 1)
                    if more:
                        for b in range(B):
                            ln.act_high(act, b, i + 1, XB, gamma_sb)

                for b in range(B):
                    ln.act_high(act, b, 0, XB, gamma_sb)
                with act.Fori(0, NBLK - 1) as i:
                    body(i, True)
                body(NBLK - 1, False)

            @block.vector
            def _(dve):
                start_counts(dve, ln.stats_done, ln.moments_done, ln.normalised, ln.low_done, rms_step, factor_done,
                             scan_done, carry_done, y_done, x_added)
                def scan_block(b, i):
                    for h in range(DC):
                        dve.wait_ge(gate_done[b], START + i * DC + h + 1)
                        dve.wait_ge(kv_ready[b], START + i * DC + h + 1)
                        dve.wait_ge(carry_done[b], START + i * DC + h)
                        nc.vector.tensor_tensor_scan(scan[:, b, h, :], gate[:, b, h, :], bank[KV[h]][:, :],
                                                     carry[:, b * DC + h:b * DC + h + 1], ALU.mult, ALU.add)\
                            .then_inc(scan_done[b], 1)
                        dve.wait_ge(scan_done[b], START + i * DC + h + 1)
                        nc.vector.tensor_copy(carry[:, b * DC + h:b * DC + h + 1],
                                              scan[:, b, h, BLK - 1:BLK]).then_inc(carry_done[b], 1)
                        dve.wait_ge(q_ready[b], START + i * DC + h + 1)
                        if h == 0:
                            dve.wait_ge(y_transposed[b], START + i)
                        nc.vector.tensor_tensor(y[:, b, h, :], bank[QB][:, :], scan[:, b, h, :],
                                                ALU.mult).then_inc(y_done[b], 1)

                def add_block(b, i):
                    dve.wait_ge(y_transposed[b], START + i + 1)
                    for j in range(2):
                        nc.vector.tensor_tensor(rows(b, i, 2 * j, 2), bank[YB[j]][:, :], rows(b, i, 2 * j, 2),
                                                ALU.add).then_inc(x_added[b], 1)

                def body(i, more):
                    if more:
                        for b in range(B):
                            a_prepare_dve(dve, b, i + 1)
                    for b in range(B):
                        scan_block(b, i)
                        if more:
                            a_factor_dve(dve, b, i + 1)
                    if more:
                        for b in range(B):
                            ln.dve_low(dve, b, i + 1, XB, gamma_sb)
                    for b in range(B):
                        add_block(b, i)

                nc.vector.memset(carry[:, :], 0.0).then_inc(carry_zero, 1)
                dve.wait_ge(carry_zero, 1)
                for b in range(B):
                    a_prepare_dve(dve, b, 0)
                for b in range(B):
                    a_factor_dve(dve, b, 0)
                for b in range(B):
                    ln.dve_low(dve, b, 0, XB, gamma_sb)
                with dve.Fori(0, NBLK - 1) as i:
                    body(i, True)
                body(NBLK - 1, False)

        wqa.close()

        def feed_forward(tag, w1t, w2t, final):
            with ExitStack() as st:
                sem, sems = semaphores(st)
                ln = LayerNorm(st, sems, tag)
                hidden = sbuf(st, f"{tag}_hidden", [P, 4, BLK])
                hid_hi = sbuf(st, f"{tag}_hid_hi", [P, B, FC, BLK], FP32R)
                hid_lo = sbuf(st, f"{tag}_hid_lo", [P, B, FC, BLK], FP32R)
                h_ready, gelu_done, hhigh_done, hlow_done = sem(f"{tag}_h"), sem(f"{tag}_gelu"), sem(f"{tag}_hhigh"), sem(f"{tag}_hlow")
                out_ready, x_added, b2_added = sems(f"{tag}_out"), sems(f"{tag}_xadd"), sems(f"{tag}_b2")
                stored, w_loaded = sem(f"{tag}_store"), sem(f"{tag}_wload")
                XB, HB, OB = (0, 1), (2, 3), ((4, 5), (6, 7))
                block = st.enter_context(nc.Block())

                @block.sync
                def _(sp):
                    if final:
                        sp.dma_start(w1t[:, :, :].rearrange("p a b -> p (a b)").bitcast(FP32), w1t_dram).then_inc(w_loaded, 16)
                        sp.dma_start(w2t[:, :, :].rearrange("p a b -> p (a b)").bitcast(FP32), w2t_dram).then_inc(w_loaded, 16)
                        with sp.Fori(0, NBLK) as i:
                            for b in range(B):
                                sp.wait_ge(x_added[b], START + (i + 1) * 2)
                                sp.dma_start(out_view[b, :, bass.ds(i * CH, CH), :],
                                             rows(b, i, 0, CH).rearrange("p (n d) -> p n d", d=D)).then_inc(stored, 16)
                        sp.wait_ge(stored, 16 * B * NBLK)

                @block.gpsimd
                def _(pool):
                    start_counts(pool, ln.vare_done, ln.rstd_done, b2_added)
                    def body(i, more):
                        if more:
                            for b in range(B):
                                ln.pool_rstd(pool, b, i + 1)
                        for b in range(B):
                            pool.wait_ge(ln.normalised[b], START + (i + 1) * CH)
                            nc.gpsimd.tensor_tensor(rows(b, i, 0, CH).rearrange("p (n d) -> p n d", d=D),
                                                    rows(b, i, 0, CH).rearrange("p (n d) -> p n d", d=D),
                                                    b2_sb[:, None, :].to_broadcast([P, CH, D]),
                                                    ALU.add).then_inc(b2_added[b], 1)
                    for b in range(B):
                        ln.pool_rstd(pool, b, 0)
                    with pool.Fori(0, NBLK - 1) as i:
                        body(i, True)
                    body(NBLK - 1, False)

                @block.tensor
                def _(pe):
                    start_counts(pe, ln.transposed, h_ready, out_ready)
                    def up(b, i):
                        pe.wait_ge(ln.low_done[b], START + (i + 1) * DC)
                        for f in range(FC):
                            pe.wait_ge(gelu_done, START + i * (2 * FC) + max(b * FC + f - 1, 0))
                            for k in range(DC):
                                w = w1t[:, k, f * P:(f + 1) * P]
                                nc.tensor.matmul(bank[HB[f % 2]][:, :], w, ln.xhi[:, b, k, :], start=(k == 0), stop=False)
                                last = nc.tensor.matmul(bank[HB[f % 2]][:, :], w, ln.xlo[:, b, k, :],
                                                        start=False, stop=(k == DC - 1))
                            last.then_inc(h_ready, 1)

                    def down(b, i):
                        pe.wait_ge(hlow_done, START + i * (2 * FC) + (b + 1) * FC)
                        pe.wait_ge(x_added[b], START + i * 2)
                        for c in range(CH):
                            dst = bank[OB[b][c // 2]][:, (c % 2) * D:(c % 2 + 1) * D]
                            for f in range(FC):
                                nc.tensor.matmul(dst, hid_hi[:, b, f, c * P:(c + 1) * P], w2t[:, f, :],
                                                 start=(f == 0), stop=False)
                                last = nc.tensor.matmul(dst, hid_lo[:, b, f, c * P:(c + 1) * P], w2t[:, f, :],
                                                        start=False, stop=(f == FC - 1))
                            if c % 2:
                                last.then_inc(out_ready[b], 1)

                    def prepare(b, i):
                        if b:
                            pe.wait_ge(ln.low_done[0], START + (i + 1) * DC)
                        else:
                            pe.wait_ge(ln.low_done[1], START + i * DC)
                        ln.pe_transpose(pe, b, i, XB)

                    def body(i, more):
                        for b in range(B):
                            up(b, i)
                        if more:
                            for b in range(B):
                                prepare(b, i + 1)
                        for b in range(B):
                            down(b, i)

                    for b in range(B):
                        prepare(b, 0)
                    if final:
                        pe.wait_ge(w_loaded, 32)
                    with pe.Fori(0, NBLK - 1) as i:
                        body(i, True)
                    body(NBLK - 1, False)

                @block.scalar
                def _(act):
                    start_counts(act, ln.high_done, gelu_done, hhigh_done)
                    def high(b, i, f):
                        act.wait_ge(gelu_done, START + i * (2 * FC) + b * FC + f + 1)
                        nc.scalar.copy(hid_hi[:, b, f, :], hidden[:, f % 4, :]).then_inc(hhigh_done, 1)

                    def body(i, more):
                        for b in range(B):
                            act.wait_ge(out_ready[b], START + i * 2)
                            for f in range(FC):
                                act.wait_ge(h_ready, START + i * (2 * FC) + b * FC + f + 1)
                                act.wait_ge(hlow_done, START + i * (2 * FC) + max(b * FC + f - 3, 0))
                                nc.scalar.activation(hidden[:, f % 4, :], bank[HB[f % 2]][:, :], ACT.Gelu,
                                                     bias=b1_sb[:, f:f + 1]).then_inc(gelu_done, 1)
                                if f:
                                    high(b, i, f - 1)
                            high(b, i, FC - 1)
                        if more:
                            for b in range(B):
                                ln.act_high(act, b, i + 1, XB)

                    for b in range(B):
                        ln.act_high(act, b, 0, XB)
                    with act.Fori(0, NBLK - 1) as i:
                        body(i, True)
                    body(NBLK - 1, False)

                @block.vector
                def _(dve):
                    start_counts(dve, ln.stats_done, ln.moments_done, ln.normalised, ln.low_done, hlow_done, x_added)
                    def body(i, more):
                        for b in range(B):
                            dve.wait_ge(out_ready[b], START + i * 2)
                            for f in range(FC):
                                dve.wait_ge(hhigh_done, START + i * (2 * FC) + b * FC + f + 1)
                                nc.vector.tensor_tensor(hid_lo[:, b, f, :], hidden[:, f % 4, :],
                                                        hid_hi[:, b, f, :].bitcast(FP32), ALU.subtract).then_inc(hlow_done, 1)
                                if more and f == 1:
                                    ln.dve_statistics(dve, b, i + 1)
                                if more and f == 5:
                                    dve.wait_ge(ln.rstd_done[b], START + i + 2)
                                    ln.dve_normalise(dve, b, i + 1)
                        if more:
                            for b in range(B):
                                ln.dve_low(dve, b, i + 1, XB)
                        for b in range(B):
                            dve.wait_ge(b2_added[b], START + i + 1)
                            for j in range(2):
                                dve.wait_ge(out_ready[b], START + i * 2 + j + 1)
                                nc.vector.tensor_tensor(rows(b, i, 2 * j, 2), bank[OB[b][j]][:, :], rows(b, i, 2 * j, 2),
                                                        ALU.add).then_inc(x_added[b], 1)

                    for b in range(B):
                        ln.dve_statistics(dve, b, 0)
                    for b in range(B):
                        dve.wait_ge(ln.rstd_done[b], START + 1)
                        ln.dve_normalise(dve, b, 0)
                    for b in range(B):
                        ln.dve_low(dve, b, 0, XB)
                    with dve.Fori(0, NBLK - 1) as i:
                        body(i, True)
                    body(NBLK - 1, False)

        feed_forward("B", w1t, w2t, False)
        tern.close()

        with ExitStack() as st:
            sem, sems = semaphores(st)
            ln = LayerNorm(st, sems, "C")
            causal = sbuf(st, "causal", [P, CH, P])
            own_head = sbuf(st, "own_head", [P, CH, P])
            v_all = sbuf(st, "v_all", [P, B, CH, H * DK])
            w_raw = sbuf(st, "w_raw", [P, 2, DC, P])
            w_hi = sbuf(st, "w_hi", [P, 2, DC, P], FP32R)
            w_lo = sbuf(st, "w_lo", [P, 2, DC, P], FP32R)
            qt = sbuf(st, "qt", [P, B, BLK])
            kt = sbuf(st, "kt", [P, B, BLK])
            krow = sbuf(st, "krow", [P, B, CH, P])
            vrow = sbuf(st, "vrow", [P, B, CH, P])
            scores = sbuf(st, "scores", [P, B, 2, CH, P])
            ut = sbuf(st, "ut", [P, B, BLK])
            urow = sbuf(st, "urow", [P, B, CH, P])
            ot_hi = sbuf(st, "ot_hi", [P, B, BLK], FP32R)
            ot_lo = sbuf(st, "ot_lo", [P, B, BLK], FP32R)
            s_state = sbuf(st, "s_state", [P, B, CH + 1, P])
            p_state = sbuf(st, "p_state", [P, B, CH + 1, P])
            s_carry = sbuf(st, "s_carry", [P, B * PAIRS * P])
            p_carry = sbuf(st, "p_carry", [P, B * PAIRS * P])

            w_loaded, w_high, w_low = sem("C_wload"), sem("C_whigh"), sem("C_wlow")
            mask_zero, masks_done, carry_zero = sem("C_maskzero"), sem("C_masks"), sem("C_zero")
            v_ready, v_stored = sem("C_v"), sem("C_vstore")
            q_ready, k_ready, qt_done, kt_done = sems("C_q"), sems("C_k"), sems("C_qt"), sems("C_kt")
            krow_ready, krow_done = sems("C_krp"), sems("C_krow")
            a_ready, a_masked, b_ready, b_masked = sems("C_a"), sems("C_am"), sems("C_b"), sems("C_bm")
            s_ready, s_masked, s_summed = sems("C_s"), sems("C_sm"), sems("C_ss")
            p_ready, p_masked, p_summed = sems("C_p"), sems("C_pm"), sems("C_ps")
            ut_ready, ut_done, urow_ready, urow_done = sems("C_utp"), sems("C_ut"), sems("C_urp"), sems("C_urow")
            o_ready, o_high, o_low = sems("C_o"), sems("C_oh"), sems("C_ol")
            out_ready, x_added = sems("C_out"), sems("C_xadd")
            s_carried, p_carried, vrow_done = sems("C_sc"), sems("C_pc"), sems("C_vr")

            QB, KB = (0, 2), (1, 3)
            KRB, SB, UB, URB, PB = (4, 5), (2, 3), (4, 5), (2, 3), (4, 5)
            AB = ((6, 7), (0, 1))
            OB, YB = (6, 0), ((7, 4), (5, 6))
            XB = ((2, 3), (0, 1))
            VB = (4, 5, 6, 7)
            V_OUT = B * CH * 2
            block = st.enter_context(nc.Block())

            def unit_loops(eng, block_start, unit):
                def one_block(i, more):
                    block_start(i)
                    with eng.Fori(0, PAIRS - 1) as p:
                        unit(i, p, i * PAIRS + p, False, True)
                    unit(i, PAIRS - 1, i * PAIRS + (PAIRS - 1), more, more)
                with eng.Fori(0, NBLK - 1) as i:
                    one_block(i, True)
                one_block(NBLK - 1, False)

            @block.sync
            def _(sp):
                start_counts(sp, w_loaded)
                with sp.Fori(0, NBLK) as i:
                    with sp.Fori(0, PAIRS) as p:
                        sp.wait_ge(w_low, START + i * PAIRS + p)
                        sp.dma_start(w_raw[:, 0:1, :, :],
                                     wq_view[:, bass.ds(p, 1)]).then_inc(w_loaded, 16)
                        sp.dma_start(w_raw[:, 1:2, :, :],
                                     wk_view[:, bass.ds(p, 1)]).then_inc(w_loaded, 16)

            @block.gpsimd
            def _(pool):
                start_counts(pool, ln.vare_done, ln.rstd_done)
                nc.gpsimd.memset(causal[:, :, :], 1.0).then_inc(mask_zero, 1)
                nc.gpsimd.memset(own_head[:, :, :], 1.0).then_inc(mask_zero, 1)
                pool.wait_ge(mask_zero, 2)
                nc.gpsimd.affine_select(out=causal[:, :, :], in_=causal[:, :, :], compare_op=ALU.is_ge, fill=0.0,
                                        base=0, pattern=[[0, CH], [1, P]], channel_multiplier=-1).then_inc(masks_done, 1)
                for h, base, step in ((0, DK - 1, -1), (1, -DK, 1)):
                    part = own_head[:, :, h * DK:(h + 1) * DK]
                    nc.gpsimd.affine_select(out=part, in_=part, compare_op=ALU.is_ge, fill=0.0, base=base,
                                            pattern=[[0, CH], [0, DK]], channel_multiplier=step).then_inc(masks_done, 1)

                for b in range(B):
                    ln.pool_rstd(pool, b, 0)
                with pool.Fori(1, NBLK) as i:
                    for b in range(B):
                        ln.pool_rstd(pool, b, i)

            @block.tensor
            def _(pe):
                start_counts(pe, ln.transposed, v_ready, q_ready, k_ready, krow_ready, a_ready, b_ready,
                             s_ready, p_ready, ut_ready, urow_ready, o_ready, out_ready)
                def prepare(b, i):
                    ln.pe_transpose(pe, b, i, XB[b])

                def block_start(i):
                    pe.wait_ge(x_added[1], START + i * PAIRS * 2)
                    for b in range(B):
                        pe.wait_ge(ln.low_done[b], START + (i + 1) * DC)
                        for c in range(CH):
                            for half in range(2):
                                n = (b * CH + c) * 2 + half
                                if n >= len(VB):
                                    pe.wait_ge(v_stored, START + i * V_OUT + n - len(VB) + 1)
                                dst = bank[VB[n % len(VB)]][:, :]
                                for k in range(DC):
                                    x_hi, x_lo = ln.xhi[:, b, k, c * P:(c + 1) * P], ln.xlo[:, b, k, c * P:(c + 1) * P]
                                    cols = slice(half * BLK, (half + 1) * BLK)
                                    nc.tensor.matmul(dst, x_hi, wv_hi[:, k, cols], start=(k == 0), stop=False)
                                    nc.tensor.matmul(dst, x_hi, wv_lo[:, k, cols], start=False, stop=False)
                                    last = nc.tensor.matmul(dst, x_lo, wv_hi[:, k, cols], start=False, stop=(k == DC - 1))
                                last.then_inc(v_ready, 1)

                def unit(i, p, u, prepare_next, more):
                    pe.wait_ge(w_low, START + u + 1)
                    for b in range(B):
                        if b == 0:
                            pe.wait_ge(o_low[1], START + u)
                        else:
                            pe.wait_ge(urow_done[1], START + u)
                        for part, dst, ready in ((0, QB[b], q_ready), (1, KB[b], k_ready)):
                            for k in range(DC):
                                last = pe_split_product(bank[dst][:, :], w_hi[:, part, k, :], w_lo[:, part, k, :],
                                                        ln.xhi[:, b, k, :], ln.xlo[:, b, k, :], k, DC - 1)
                            last.then_inc(ready[b], 1)
                    pe.wait_ge(v_stored, START + (i + 1) * V_OUT)
                    for b in range(B):
                        pe.wait_ge(kt_done[b], START + u + 1)
                        pe.wait_ge(x_added[b], START + u * 2)
                        for c in range(CH):
                            last = nc.tensor.transpose(bank[KRB[b]][:, c * P:(c + 1) * P], kt[:, b, c * P:(c + 1) * P], ident[:, :])
                        last.then_inc(krow_ready[b], 1)
                        pe.wait_ge(qt_done[b], START + u + 1)
                        if b == 0:
                            pe.wait_ge(x_added[1], START + u * 2)
                        for h in range(2):
                            hd = slice(h * DK, (h + 1) * DK)
                            for c in range(CH):
                                tok = slice(c * P, (c + 1) * P)
                                last = nc.tensor.matmul(bank[AB[b][h]][:, tok], kt[hd, b, tok], qt[hd, b, tok], start=True, stop=True)
                            last.then_inc(a_ready[b], 1)
                    for b in range(B):
                        pe.wait_ge(krow_done[b], START + u + 1)
                        for c in range(CH):
                            last = nc.tensor.matmul(bank[SB[b]][:, c * P:(c + 1) * P], krow[:, b, c, :], krow[:, b, c, :],
                                                    start=True, stop=True)
                        last.then_inc(s_ready[b], 1)
                    for b in range(B):
                        pe.wait_ge(s_carried[b], START + u + 1)
                        pe.wait_ge(s_summed[b], START + (u + 1) * CH)
                        for c in range(CH):
                            tok = slice(c * P, (c + 1) * P)
                            nc.tensor.matmul(bank[UB[b]][:, tok], s_state[:, b, c, :], qt[:, b, tok],
                                             start=(c == 0), stop=False, skip_group_check=True)
                        pe.wait_ge(a_masked[b], START + (u + 1) * 2)
                        for c in range(CH):
                            tok = slice(c * P, (c + 1) * P)
                            for h in range(2):
                                hd = slice(h * DK, (h + 1) * DK)
                                last = nc.tensor.matmul(bank[UB[b]][hd, tok], krow[:, b, c, hd], scores[:, b, h, c, :],
                                                        start=False, stop=(c == CH - 1), skip_group_check=True)
                        last.then_inc(ut_ready[b], 1)
                    for b in range(B):
                        pe.wait_ge(ut_done[b], START + u + 1)
                        for h in range(2):
                            hd = slice(h * DK, (h + 1) * DK)
                            for c in range(CH):
                                tok = slice(c * P, (c + 1) * P)
                                last = nc.tensor.matmul(bank[AB[b][h]][:, tok], ut[hd, b, tok], qt[hd, b, tok], start=True, stop=True)
                            last.then_inc(b_ready[b], 1)
                    for b in range(B):
                        pe.wait_ge(s_masked[b], START + u + 1)
                        for c in range(CH):
                            last = nc.tensor.transpose(bank[URB[b]][:, c * P:(c + 1) * P], ut[:, b, c * P:(c + 1) * P], ident[:, :])
                        last.then_inc(urow_ready[b], 1)
                    for b in range(B):
                        pe.wait_ge(urow_done[b], START + u + 1)
                        pe.wait_ge(vrow_done[b], START + u + 1)
                        for c in range(CH):
                            last = nc.tensor.matmul(bank[PB[b]][:, c * P:(c + 1) * P], urow[:, b, c, :], vrow[:, b, c, :],
                                                    start=True, stop=True)
                        last.then_inc(p_ready[b], 1)
                    for b in range(B):
                        pe.wait_ge(b_masked[b], START + (u + 1) * 2)
                        pe.wait_ge(p_carried[b], START + u + 1)
                        pe.wait_ge(p_summed[b], START + (u + 1) * CH)
                        for c in range(CH):
                            tok = slice(c * P, (c + 1) * P)
                            nc.tensor.matmul(bank[OB[b]][:, tok], p_state[:, b, c, :], qt[:, b, tok],
                                             start=(c == 0), stop=False, skip_group_check=True)
                        for c in range(CH):
                            tok = slice(c * P, (c + 1) * P)
                            for h in range(2):
                                hd = slice(h * DK, (h + 1) * DK)
                                last = nc.tensor.matmul(bank[OB[b]][hd, tok], vrow[:, b, c, hd], scores[:, b, h, c, :],
                                                        start=False, stop=(c == CH - 1), skip_group_check=True)
                        last.then_inc(o_ready[b], 1)
                    for b in range(B):
                        pe.wait_ge(o_low[b], START + u + 1)
                        pe.wait_ge(p_masked[b], START + u + 1)
                        if prepare_next:
                            if b:
                                pe.wait_ge(o_low[1], START + u + 1)
                            prepare(b, i + 1)
                        for c in range(CH):
                            tok = slice(c * P, (c + 1) * P)
                            dst = bank[YB[b][c // 2]][:, (c % 2) * D:(c % 2 + 1) * D]
                            w = [x[:, bass.ds(p * D, D)] for x in (wo_hi, wo_lo)]
                            nc.tensor.matmul(dst, ot_hi[:, b, tok], w[0], start=True, stop=False)
                            nc.tensor.matmul(dst, ot_hi[:, b, tok], w[1], start=False, stop=False)
                            last = nc.tensor.matmul(dst, ot_lo[:, b, tok], w[0], start=False, stop=True)
                            if c % 2:
                                last.then_inc(out_ready[b], 1)

                for b in range(B):
                    prepare(b, 0)
                unit_loops(pe, block_start, unit)

            @block.scalar
            def _(act):
                start_counts(act, ln.high_done, w_high, v_stored, qt_done, kt_done, krow_done, ut_done,
                             urow_done, o_high)
                def split_weights(u):
                    act.wait_ge(w_loaded, START + (u + 1) * 32)
                    act.wait_ge(k_ready[1], START + u)
                    nc.scalar.copy(w_hi[:, :, :, :], w_raw[:, :, :, :]).then_inc(w_high, 1)

                def block_start(i):
                    act.wait_ge(vrow_done[1], START + i * PAIRS)
                    for n in range(V_OUT):
                        act.wait_ge(v_ready, START + i * V_OUT + n + 1)
                        b, c, half = n // (2 * CH), n // 2 % CH, n % 2
                        nc.scalar.copy(v_all[:, b, c, half * BLK:(half + 1) * BLK], bank[VB[n % len(VB)]][:, :])\
                            .then_inc(v_stored, 1)

                def unit(i, p, u, prepare_next, more):
                    for b in range(B):
                        act.wait_ge(q_ready[b], START + u + 1)
                        act.wait_ge(o_ready[b], START + u)
                        nc.scalar.copy(qt[:, b, :], bank[QB[b]][:, :]).then_inc(qt_done[b], 1)
                        act.wait_ge(k_ready[b], START + u + 1)
                        act.wait_ge(a_ready[b], START + u * 2)
                        nc.scalar.copy(kt[:, b, :], bank[KB[b]][:, :]).then_inc(kt_done[b], 1)
                    for b in range(B):
                        act.wait_ge(krow_ready[b], START + u + 1)
                        act.wait_ge(ut_ready[b], START + u)
                        nc.scalar.copy(krow[:, b, :, :].rearrange("p c d -> p (c d)"), bank[KRB[b]][:, :]).then_inc(krow_done[b], 1)
                    if more:
                        split_weights(u + 1)
                    for b in range(B):
                        act.wait_ge(ut_ready[b], START + u + 1)
                        nc.scalar.copy(ut[:, b, :], bank[UB[b]][:, :]).then_inc(ut_done[b], 1)
                    for b in range(B):
                        act.wait_ge(urow_ready[b], START + u + 1)
                        act.wait_ge(p_ready[b], START + u)
                        nc.scalar.copy(urow[:, b, :, :].rearrange("p c d -> p (c d)"), bank[URB[b]][:, :]).then_inc(urow_done[b], 1)
                    for b in range(B):
                        act.wait_ge(o_ready[b], START + u + 1)
                        act.wait_ge(out_ready[b], START + u * 2)
                        nc.scalar.copy(ot_hi[:, b, :], bank[OB[b]][:, :]).then_inc(o_high[b], 1)
                    if prepare_next:
                        for b in range(B):
                            ln.act_high(act, b, i + 1, XB[b])

                for b in range(B):
                    ln.act_high(act, b, 0, XB[b])
                split_weights(0)
                unit_loops(act, block_start, unit)

            @block.vector
            def _(dve):
                start_counts(dve, ln.stats_done, ln.moments_done, ln.normalised, ln.low_done, w_low, a_masked, b_masked,
                             s_masked, s_summed, s_carried, p_masked, p_summed, p_carried, vrow_done, o_low, x_added)
                def split_weights(u):
                    dve.wait_ge(w_high, START + u + 1)
                    nc.vector.tensor_tensor(w_lo[:, :, :, :], w_raw[:, :, :, :], w_hi[:, :, :, :].bitcast(FP32),
                                            ALU.subtract).then_inc(w_low, 1)

                def mask_scores(b, u, ready, masked):
                    for h in range(2):
                        dve.wait_ge(ready[b], START + u * 2 + h + 1)
                        nc.vector.tensor_tensor(scores[:, b, h, :, :], bank[AB[b][h]][:, :].rearrange("p (c d) -> p c d", c=CH),
                                                causal[:, :, :], ALU.mult).then_inc(masked[b], 1)

                def sum_states(b, p, u, SBANK, state, carry, ready, masked, summed, carried):
                    dve.wait_ge(ready[b], START + u + 1)
                    nc.vector.tensor_tensor(state[:, b, 1:, :], bank[SBANK[b]][:, :].rearrange("p (c d) -> p c d", c=CH),
                                            own_head[:, :, :], ALU.mult).then_inc(masked[b], 1)
                    dve.wait_ge(masked[b], START + u + 1)
                    dve.wait_ge(carried[b], START + u + 1)
                    for c in range(CH):
                        if c:
                            dve.wait_ge(summed[b], START + u * CH + c)
                        dst = state[:, b, c + 1, :] if c < CH - 1 else carry[:, bass.ds((p + b * PAIRS) * P, P)]
                        nc.vector.tensor_tensor(dst, state[:, b, c + 1, :], state[:, b, c, :], ALU.add).then_inc(summed[b], 1)

                def block_start(i):
                    pass

                def unit(i, p, u, prepare_next, more):
                    for b in range(B):
                        dve.wait_ge(s_summed[b], START + u * CH)
                        dve.wait_ge(ut_ready[b], START + u)
                        nc.vector.tensor_copy(s_state[:, b, 0, :], s_carry[:, bass.ds((p + b * PAIRS) * P, P)])\
                            .then_inc(s_carried[b], 1)
                        dve.wait_ge(p_summed[b], START + u * CH)
                        dve.wait_ge(o_ready[b], START + u)
                        nc.vector.tensor_copy(p_state[:, b, 0, :], p_carry[:, bass.ds((p + b * PAIRS) * P, P)])\
                            .then_inc(p_carried[b], 1)
                        dve.wait_ge(v_stored, START + (i + 1) * V_OUT)
                        nc.vector.tensor_copy(vrow[:, b, :, :], v_all[:, b, :, bass.ds(p * P, P)]).then_inc(vrow_done[b], 1)
                    for b in range(B):
                        mask_scores(b, u, a_ready, a_masked)
                    if more:
                        split_weights(u + 1)
                    for b in range(B):
                        sum_states(b, p, u, SB, s_state, s_carry, s_ready, s_masked, s_summed, s_carried)
                    if prepare_next:
                        for b in range(B):
                            ln.dve_statistics(dve, b, i + 1)
                    for b in range(B):
                        dve.wait_ge(ut_ready[b], START + u + 1)
                        mask_scores(b, u, b_ready, b_masked)
                    for b in range(B):
                        sum_states(b, p, u, PB, p_state, p_carry, p_ready, p_masked, p_summed, p_carried)
                    if prepare_next:
                        for b in range(B):
                            dve.wait_ge(ln.rstd_done[b], START + i + 2)
                            ln.dve_normalise(dve, b, i + 1)
                    for b in range(B):
                        dve.wait_ge(o_high[b], START + u + 1)
                        nc.vector.tensor_tensor(ot_lo[:, b, :], bank[OB[b]][:, :], ot_hi[:, b, :].bitcast(FP32),
                                                ALU.subtract).then_inc(o_low[b], 1)
                    for b in range(B):
                        if prepare_next:
                            ln.dve_low(dve, b, i + 1, XB[b])
                        for j in range(2):
                            dve.wait_ge(out_ready[b], START + u * 2 + j + 1)
                            nc.vector.tensor_tensor(rows(b, i, 2 * j, 2), bank[YB[b][j]][:, :], rows(b, i, 2 * j, 2),
                                                    ALU.add).then_inc(x_added[b], 1)

                nc.vector.memset(s_carry[:, :], 0.0).then_inc(carry_zero, 1)
                nc.vector.memset(p_carry[:, :], 0.0).then_inc(carry_zero, 1)
                for b in range(B):
                    ln.dve_statistics(dve, b, 0)
                for b in range(B):
                    dve.wait_ge(ln.rstd_done[b], START + 1)
                    ln.dve_normalise(dve, b, 0)
                for b in range(B):
                    ln.dve_low(dve, b, 0, XB[b])
                split_weights(0)
                dve.wait_ge(masks_done, 3)
                unit_loops(dve, block_start, unit)

        with ExitStack() as st:
            w1t = sbuf(st, "w1t_d", [P, DC, FF], FP32R)
            w2t = sbuf(st, "w2t_d", [P, FC, D], FP32R)
            feed_forward("D", w1t, w2t, True)


_INS = ["L0_attn_a_x", "L0_attn_a_gamma", "L0_attn_a_w_qkva", "L0_attn_b_W_q", "L0_attn_b_W_k", "L0_attn_b_W_v",
        "L0_attn_b_W_o", "L0_ffn_W1", "L0_ffn_b1", "L0_ffn_W2", "L0_ffn_b2"]
_OUTS = [((B, T, D), "float32")]


def kernel(**inputs):
    import numpy as _np
    import concourse.bacc as _bacc
    from concourse import mybir as _mybir
    from concourse.bass_utils import run_bass_kernel_spmd as _run

    nc = _bacc.Bacc("TRN2", target_bir_lowering=False, num_devices=1)
    arrays, args = {}, []
    for name in _INS:
        a = _np.ascontiguousarray(inputs[name])
        arrays[f"in_{name}_dram"] = a
        args.append(nc.dram_tensor(f"in_{name}_dram", a.shape, _mybir.dt.from_np(a.dtype), kind="ExternalInput").ap())
    for i, (shape, dtype) in enumerate(_OUTS):
        dt = _mybir.dt.from_np(_np.dtype(dtype))
        args.append(nc.dram_tensor(f"out_{i}_dram", shape, dt, kind="ExternalOutput").ap())
    hybrid_kernel(nc, *args)
    r = _run(nc, [arrays], core_ids=[0])
    got = tuple(r.results[0][f"out_{i}_dram"] for i in range(len(_OUTS)))
    return got[0]
```

```python
import concourse.bass as bass
from concourse import mybir
from contextlib import ExitStack

FP32 = mybir.dt.float32
FP32R = mybir.dt.float32r
ALU = mybir.AluOpType
ACT = mybir.ActivationFunctionType
AX = mybir.AxisListType

START = 1

P = 128
B, T, D = 2, 2048, 256
DC = D // P
BLK = 512
CH = BLK // P
NBLK = T // BLK
TILES = T // P
FF = 1024
FC = FF // P
H, DK = 16, 64
PAIRS = H // 2
QKVA = 3 * D
LN_EPS = 1e-5
RMS_EPS = 1e-12


def hybrid_kernel(nc, x_d, gamma_d, wqkva_d, wq_d, wk_d, wv_d, wo_d, w1_d, b1_d, w2_d, b2_d, out_d):
    x_view = x_d.rearrange("b (n p) d -> b p n d", p=P)
    out_view = out_d.rearrange("b (n p) d -> b p n d", p=P)
    wq_view = wq_d.rearrange("(k p) (n c) -> p n k c", p=P, c=P)
    wk_view = wk_d.rearrange("(k p) (n c) -> p n k c", p=P, c=P)

    outer = ExitStack()
    with outer:
        def sbuf(stack, name, shape, dtype=FP32):
            return stack.enter_context(nc.sbuf_tensor(name, shape, dtype))

        def semaphores(stack):
            used = []

            @stack.callback
            def _():
                with nc.Block() as block:
                    @block.gpsimd
                    def _(pool):
                        nums = sorted(s.num for s in used)
                        starts = [n for n in nums if n - 1 not in nums]
                        ends = [n + 1 for n in nums if n + 1 not in nums]
                        for first, end in zip(starts, ends):
                            pool.sem_clear(range(first, end))
                for s in used:
                    nc.release_semaphore(s)

            def sem(name):
                used.append(nc.alloc_semaphore(name))
                return used[-1]

            def sems(name):
                return [sem(f"{name}{b}") for b in range(B)]
            return sem, sems

        xres = sbuf(outer, "xres", [P, B * TILES * D])
        ident = sbuf(outer, "ident", [P, P])
        wv_hi = sbuf(outer, "wv_hi", [P, DC, H * DK], FP32R)
        wv_lo = sbuf(outer, "wv_lo", [P, DC, H * DK], FP32R)
        wo_hi = sbuf(outer, "wo_hi", [P, PAIRS * D], FP32R)
        wo_lo = sbuf(outer, "wo_lo", [P, PAIRS * D], FP32R)
        b1_sb = sbuf(outer, "b1_sb", [P, FC])
        b2_sb = sbuf(outer, "b2_sb", [P, D])
        gamma_sb = sbuf(outer, "gamma_sb", [P, DC])
        ln_stats = sbuf(outer, "ln_stats", [P, B, CH, 6])
        ln_moments = sbuf(outer, "ln_moments", [P, B, CH, 2])
        ln_vare = sbuf(outer, "ln_vare", [P, B, CH])
        ln_rstd = sbuf(outer, "ln_rstd", [P, B, CH])
        ln_filler = sbuf(outer, "ln_filler", [P, 1])
        ln_eps = sbuf(outer, "ln_eps", [P, CH])
        minus_half = sbuf(outer, "minus_half", [P, CH])
        plus_half = sbuf(outer, "plus_half", [P, CH])
        bank = [outer.enter_context(nc.psum_tensor(f"bank{i}", [P, BLK], FP32)) for i in range(8)]
        w1t_dram = nc.dram_tensor("w1t_scratch", (P, DC * FF), FP32, kind="Internal").ap()
        w2t_dram = nc.dram_tensor("w2t_scratch", (P, FC * D), FP32, kind="Internal").ap()

        def start_counts(eng, *semaphores_of_eng):
            for s in semaphores_of_eng:
                for one in (s if isinstance(s, list) else [s]):
                    eng.sem_inc(one, START)

        def rows(b, i, c=0, n=1):
            return xres[:, bass.ds((i * CH + (b * TILES + c)) * D, n * D)]

        class LayerNorm:
            def __init__(self, stack, sems):
                self.xn = sbuf(stack, "ln_xn", [P, B, CH, D])
                self.xhi = sbuf(stack, "ln_xhi", [P, B, DC, BLK], FP32R)
                self.xlo = sbuf(stack, "ln_xlo", [P, B, DC, BLK], FP32R)
                self.stats_done = sems("ln_stats_done")
                self.moments_done = sems("ln_moments_done")
                self.vare_done = sems("ln_vare_done")
                self.rstd_done = sems("ln_rstd_done")
                self.normalised = sems("ln_normalised")
                self.transposed = sems("ln_transposed")
                self.high_done = sems("ln_high_done")
                self.low_done = sems("ln_low_done")

            def dve_statistics(self, dve, b, i, n):
                for c in range(CH):
                    nc.vector.bn_stats(ln_stats[:, b, c, :], rows(b, i, c)).then_inc(self.stats_done[b], 1)
                dve.wait_ge(self.stats_done[b], START + (n + 1) * CH)
                nc.vector.memset(ln_filler[:, :], 0.0)
                for c in range(CH):
                    nc.vector.bn_aggr(ln_moments[:, b, c, :], ln_stats[:, b, c, :]).then_inc(self.moments_done[b], 1)

            def pool_rstd(self, pool, b, n):
                pool.wait_ge(self.moments_done[b], START + (n + 1) * CH)
                nc.gpsimd.tensor_tensor(ln_vare[:, b, :], ln_moments[:, b, :, 1], ln_eps[:, :],
                                        ALU.add).then_inc(self.vare_done[b], 1)
                pool.wait_ge(self.vare_done[b], START + n + 1)
                nc.gpsimd.tensor_tensor(ln_rstd[:, b, :], ln_vare[:, b, :], minus_half[:, :],
                                        ALU.pow).then_inc(self.rstd_done[b], 1)

            def dve_normalise(self, dve, b, i, n, factor):
                dve.wait_ge(self.transposed[b], START + n * DC)
                for c in range(CH):
                    nc.vector.tensor_scalar(self.xn[:, b, c, :], rows(b, i, c), ln_moments[:, b, c, 0:1],
                                            factor[:, b, c:c + 1], ALU.subtract, ALU.mult)\
                        .then_inc(self.normalised[b], 1)

            def pe_transpose(self, pe, b, n, banks):
                pe.wait_ge(self.normalised[b], START + (n + 1) * CH)
                for k in range(DC):
                    for c in range(CH):
                        last = nc.tensor.transpose(bank[banks[k]][:, c * P:(c + 1) * P],
                                                   self.xn[:, b, c, k * P:(k + 1) * P], ident[:, :])
                    last.then_inc(self.transposed[b], 1)

            def act_high(self, act, b, n, banks, scale=None):
                for k in range(DC):
                    act.wait_ge(self.transposed[b], START + n * DC + k + 1)
                    nc.scalar.activation(self.xhi[:, b, k, :], bank[banks[k]][:, :], ACT.Identity,
                                         scale=1.0 if scale is None else scale[:, k:k + 1])\
                        .then_inc(self.high_done[b], 1)

            def dve_low(self, dve, b, n, banks, scale=None):
                for k in range(DC):
                    dve.wait_ge(self.high_done[b], START + n * DC + k + 1)
                    if scale is None:
                        nc.vector.tensor_tensor(self.xlo[:, b, k, :], bank[banks[k]][:, :],
                                                self.xhi[:, b, k, :].bitcast(FP32), ALU.subtract)\
                            .then_inc(self.low_done[b], 1)
                    else:
                        nc.vector.scalar_tensor_tensor(self.xlo[:, b, k, :], bank[banks[k]][:, :],
                                                       scale[:, k:k + 1], self.xhi[:, b, k, :].bitcast(FP32),
                                                       ALU.mult, ALU.subtract).then_inc(self.low_done[b], 1)

        ln = LayerNorm(outer, semaphores(outer)[1])

        def pe_split_product(out, w_hi, w_lo, x_hi, x_lo, k, last_k):
            nc.tensor.matmul(out, w_hi, x_hi, start=(k == 0), stop=False)
            nc.tensor.matmul(out, w_hi, x_lo, start=False, stop=False)
            return nc.tensor.matmul(out, w_lo, x_hi, start=False, stop=(k == last_k))

        tern = outer.enter_context(ExitStack())
        w1t = sbuf(tern, "w1t", [P, DC, FF], FP32R)
        w2t = sbuf(tern, "w2t", [P, FC, D], FP32R)
        wqa = tern.enter_context(ExitStack())
        wa_hi = sbuf(wqa, "wa_hi", [P, DC, QKVA], FP32R)
        wa_lo = sbuf(wqa, "wa_lo", [P, DC, QKVA], FP32R)

        with ExitStack() as st:
            sem, sems = semaphores(st)
            wa_nat = sbuf(st, "wa_nat", [P, QKVA // P, D])
            w1_nat = sbuf(st, "w1_nat", [P, FC, D])
            w2_nat = sbuf(st, "w2_nat", [P, DC, FF])
            below = sbuf(st, "below", [P, FC * D])
            wv_raw = sbuf(st, "wv_raw", [P, DC, H * DK])
            wo_raw = sbuf(st, "wo_raw", [P, PAIRS * D])
            ones = sbuf(st, "ones", [P, P])
            abs_sum = sbuf(st, "abs_sum", [P, 2])
            thr = sbuf(st, "thr", [P, 2])
            minus_thr = sbuf(st, "minus_thr", [P, 2])
            x_loaded = [sem(f"x_loaded_{which}") for which in ("first", "second", "rest")]
            wa_loaded, w12_loaded, wvo_loaded = sem("wa_loaded"), sem("w12_loaded"), sem("wvo_loaded")
            gamma_loaded, bias_loaded = sem("gamma_loaded"), sem("bias_loaded")
            ident_zero, ident_done, consts_done = sem("ident_zero"), sem("ident_done"), sem("consts_done")
            wa_transposed, wa_high, wa_low = sem("wa_transposed"), sem("wa_high"), sem("wa_low")
            abs_done, sum_done, thr_step, below_done, tern_done = sem("abs_done"), sem("sum_done"), sem("thr_step"), sem("below_done"), sem("tern_done")
            wt_ready, wt_done = sem("wt_ready"), sem("wt_done")
            wvo_high, wvo_low = sem("wvo_high"), sem("wvo_low")

            rms_std = sbuf(st, "rms_std", [P, B, CH])
            rms_norm = sbuf(st, "rms_norm", [P, B, CH])
            rms_factor = sbuf(st, "rms_factor", [P, B, CH])
            gate = sbuf(st, "gate", [P, B, DC, BLK])
            scan = sbuf(st, "scan", [P, B, DC, BLK])
            carry = sbuf(st, "carry", [P, B * DC])
            y = sbuf(st, "y", [P, B, DC, BLK])
            std_done, rms_step, factor_done = sems("A_std"), sems("A_rmsstep"), sems("A_factor")
            kv_ready, a_ready, q_ready = sems("A_kv"), sems("A_a"), sems("A_q")
            gate_done, scan_done, carry_done, y_done = sems("A_gate"), sems("A_scan"), sems("A_carry"), sems("A_y")
            y_transposed, x_added, carry_zero = sems("A_yt"), sems("A_xadd"), sem("A_zero")
            XB, KV, AB, QB, YB = (0, 1), (2, 3), 4, 5, (6, 7)
            WAB, SUMB = (2, 3, 4), 6
            WT = 2 * DC * FF // BLK
            flat = "p a b -> p (a b)"
            block = st.enter_context(nc.Block())

            def stage_loop(eng, body):
                body(0, True, False)
                with eng.Fori(1, NBLK - 1) as i:
                    body(i, False, False)
                body(NBLK - 1, False, True)

            @block.sync
            def _(sp):
                for i in range(NBLK):
                    for b in range(B):
                        sp.dma_start(rows(b, i, 0, CH).rearrange("p (n d) -> p n d", d=D),
                                     x_view[b, :, i * CH:(i + 1) * CH, :]).then_inc(x_loaded[min(i, 2)], 16)

            @block.gpsimd
            def _(pool):
                start_counts(pool, ln.vare_done, ln.rstd_done, std_done)
                nc.gpsimd.memset(ident[:, :], 0.0).then_inc(ident_zero, 1)
                nc.gpsimd.memset(ones[:, :], 1.0).then_inc(consts_done, 1)
                nc.gpsimd.memset(minus_half[:, :], -0.5).then_inc(consts_done, 1)
                nc.gpsimd.memset(plus_half[:, :], 0.5).then_inc(consts_done, 1)
                nc.gpsimd.memset(ln_eps[:, :], LN_EPS).then_inc(consts_done, 1)
                pool.wait_ge(ident_zero, 1)
                nc.gpsimd.affine_select(out=ident[:, :], in_=ident[:, :], compare_op=ALU.not_equal, fill=1.0,
                                        base=0, pattern=[[-1, P]], channel_multiplier=1).then_inc(ident_done, 1)
                pool.wait_ge(consts_done, 4)

                def prepare(n):
                    for b in range(B):
                        ln.pool_rstd(pool, b, n)
                        nc.gpsimd.tensor_tensor(rms_std[:, b, :], ln_moments[:, b, :, 1], plus_half[:, :],
                                                ALU.pow).then_inc(std_done[b], 1)
                prepare(0)
                with pool.Fori(1, NBLK) as i:
                    prepare(i)
                for b in range(B):
                    ln.pool_rstd(pool, b, NBLK)

            @block.tensor
            def _(pe):
                start_counts(pe, ln.transposed, kv_ready, a_ready, q_ready, y_transposed)

                def transpose_wa():
                    for m in range(DC * QKVA // P):
                        k, r = m // (QKVA // P), m % (QKVA // P)
                        last = nc.tensor.transpose(bank[WAB[m // 4]][:, (m % 4) * P:(m % 4 + 1) * P],
                                                   wa_nat[:, r, k * P:(k + 1) * P], ident[:, :])
                        if m % 4 == 3:
                            last.then_inc(wa_transposed, 1)

                def transpose_ternary(g):
                    pe.wait_ge(tern_done, 1 if g < WT // 2 else 2)
                    if g < 2:
                        pe.wait_ge(ln.low_done[1], START + NBLK * DC)
                    else:
                        pe.wait_ge(wt_done, g - 1)
                    for m in range(4):
                        if g < WT // 2:
                            k, r = g // 2, (g % 2) * 4 + m
                            src = w1_nat[:, r, k * P:(k + 1) * P]
                        else:
                            f, k = 2 * (g - WT // 2) + m // 2, m % 2
                            src = w2_nat[:, k, f * P:(f + 1) * P]
                        last = nc.tensor.transpose(bank[XB[g % 2]][:, m * P:(m + 1) * P], src, ident[:, :])
                    last.then_inc(wt_ready, 1)

                def project(b, i):
                    pe.wait_ge(ln.low_done[b], START + (i + 1) * DC)
                    other = 1 - b
                    for h in range(DC):
                        for what, dst, part, ready in (("kv", KV[h], 1, kv_ready), ("a", AB, 2, a_ready), ("q", QB, 0, q_ready)):
                            if what == "kv":
                                if b:
                                    pe.wait_ge(scan_done[other], START + i * DC + h + 1)
                                else:
                                    pe.wait_ge(scan_done[other], START + i * DC)
                            elif what == "a":
                                if h:
                                    pe.wait_ge(gate_done[b], START + i * DC + 1)
                                else:
                                    pe.wait_ge(gate_done[other], START + (i + b) * DC)
                            else:
                                if h:
                                    pe.wait_ge(y_done[b], START + i * DC + 1)
                                else:
                                    pe.wait_ge(y_done[other], START + (i + b) * DC)
                            for k in range(DC):
                                cols = slice(part * D + h * P, part * D + (h + 1) * P)
                                last = pe_split_product(bank[dst][:, :], wa_hi[:, k, cols], wa_lo[:, k, cols],
                                                        ln.xhi[:, b, k, :], ln.xlo[:, b, k, :], k, DC - 1)
                            last.then_inc(ready[b], 1)

                def transpose_y(b, i):
                    for h in range(DC):
                        pe.wait_ge(y_done[b], START + i * DC + h + 1)
                        if h == 0:
                            pe.wait_ge(x_added[1 - b], START + (i + b) * 2)
                        for c in range(CH):
                            last = nc.tensor.transpose(bank[YB[c // 2]][:, (c % 2) * D + h * P:(c % 2) * D + (h + 1) * P],
                                                       y[:, b, h, c * P:(c + 1) * P], ident[:, :])
                    last.then_inc(y_transposed[b], 1)

                def prepare(b, n):
                    if b:
                        pe.wait_ge(ln.low_done[0], START + (n + 1) * DC)
                    else:
                        pe.wait_ge(ln.low_done[1], START + n * DC)
                    ln.pe_transpose(pe, b, n, XB)

                def body(i, first, last):
                    for b in range(B):
                        project(b, i)
                        if last:
                            for g in range(b * WT // B, (b + 1) * WT // B):
                                transpose_ternary(g)
                    if first:
                        pe.wait_ge(abs_done, 2)
                        nc.tensor.matmul(bank[SUMB][:, 0:2], ones[:, :], abs_sum[:, :], start=True, stop=True)\
                            .then_inc(sum_done, 1)
                    if last:
                        pe.wait_ge(wt_done, WT)
                    for b in range(B):
                        prepare(b, i + 1)
                    if first:
                        pe.wait_ge(thr_step, 1)
                    for b in range(B):
                        transpose_y(b, i)

                pe.wait_ge(consts_done, 4)
                pe.wait_ge(ident_done, 1)
                pe.wait_ge(wa_loaded, 16)
                transpose_wa()
                for b in range(B):
                    prepare(b, 0)
                pe.wait_ge(wa_low, len(WAB))
                stage_loop(pe, body)

            @block.scalar
            def _(act):
                start_counts(act, ln.high_done, gate_done)
                act.dma_start(wa_nat[:, :, :], wqkva_d.rearrange("(n p) d -> p n d", p=P)).then_inc(wa_loaded, 16)
                act.dma_start(gamma_sb[:, :], gamma_d.rearrange("(n p) -> p n", p=P), allow_slow_non_contiguous=True).then_inc(gamma_loaded, 16)
                act.dma_start(w1_nat[:, :, :], w1_d.rearrange("(n p) d -> p n d", p=P)).then_inc(w12_loaded, 16)
                act.dma_start(w2_nat[:, :, :], w2_d.rearrange("(n p) d -> p n d", p=P)).then_inc(w12_loaded, 16)
                act.dma_start(wv_raw[:, :, :], wv_d.rearrange("(k p) c -> p k c", p=P)).then_inc(wvo_loaded, 16)
                act.dma_start(wo_raw[:, :].rearrange("p (n d) -> p n d", d=D),
                              wo_d.rearrange("(n p) d -> p n d", p=P)).then_inc(wvo_loaded, 16)
                act.dma_start(b1_sb[:, :], b1_d.rearrange("(n p) -> p n", p=P), allow_slow_non_contiguous=True).then_inc(bias_loaded, 16)
                act.dma_start(b2_sb[:, :], b2_d.partition_broadcast(P)).then_inc(bias_loaded, 16)

                def body(i, first, last):
                    for b in range(B):
                        for h in range(DC):
                            act.wait_ge(a_ready[b], START + i * DC + h + 1)
                            act.wait_ge(scan_done[b], START + i * DC)
                            nc.scalar.activation(gate[:, b, h, :], bank[AB][:, :], ACT.Sigmoid).then_inc(gate_done[b], 1)
                        if last:
                            for g in range(b * WT // B, (b + 1) * WT // B):
                                act.wait_ge(wt_ready, g + 1)
                                dst = (w1t if g < WT // 2 else w2t)[:, :, :].rearrange(flat)
                                cols = slice(g % (WT // 2) * BLK, (g % (WT // 2) + 1) * BLK)
                                nc.scalar.copy(dst[:, cols], bank[XB[g % 2]][:, :]).then_inc(wt_done, 1)
                    if first:
                        act.wait_ge(wvo_loaded, 32)
                        nc.scalar.copy(wv_hi[:, :, :], wv_raw[:, :, :]).then_inc(wvo_high, 1)
                        nc.scalar.copy(wo_hi[:, :], wo_raw[:, :]).then_inc(wvo_high, 1)
                    for b in range(B):
                        ln.act_high(act, b, i + 1, XB, None if last else gamma_sb)

                for n in range(len(WAB)):
                    act.wait_ge(wa_transposed, n + 1)
                    nc.scalar.copy(wa_hi[:, :, :].rearrange(flat)[:, n * BLK:(n + 1) * BLK], bank[WAB[n]][:, :]).then_inc(wa_high, 1)
                act.wait_ge(gamma_loaded, 16)
                for b in range(B):
                    ln.act_high(act, b, 0, XB, gamma_sb)
                stage_loop(act, body)
                act.wait_ge(bias_loaded, 32)

            @block.vector
            def _(dve):
                start_counts(dve, ln.stats_done, ln.moments_done, ln.normalised, ln.low_done, rms_step, factor_done,
                             scan_done, carry_done, y_done, x_added)

                def normalise(b, i):
                    dve.wait_ge(std_done[b], START + i + 1)
                    nc.vector.scalar_tensor_tensor(rms_norm[:, b, :], ln_rstd[:, b, :], float(D) ** 0.5, rms_std[:, b, :],
                                                   ALU.mult, ALU.mult).then_inc(rms_step[b], 1)
                    dve.wait_ge(rms_step[b], START + 3 * i + 1)
                    nc.vector.tensor_scalar(rms_norm[:, b, :], rms_norm[:, b, :], RMS_EPS, None, ALU.max).then_inc(rms_step[b], 1)
                    dve.wait_ge(rms_step[b], START + 3 * i + 2)
                    nc.vector.reciprocal(rms_norm[:, b, :], rms_norm[:, b, :]).then_inc(rms_step[b], 1)
                    dve.wait_ge(rms_step[b], START + 3 * i + 3)
                    nc.vector.scalar_tensor_tensor(rms_factor[:, b, :], ln_rstd[:, b, :], float(D) ** 0.5, rms_norm[:, b, :],
                                                   ALU.mult, ALU.mult).then_inc(factor_done[b], 1)
                    dve.wait_ge(factor_done[b], START + i + 1)
                    ln.dve_normalise(dve, b, i, i, rms_factor)

                def scan_block(b, i):
                    for h in range(DC):
                        dve.wait_ge(gate_done[b], START + i * DC + h + 1)
                        dve.wait_ge(kv_ready[b], START + i * DC + h + 1)
                        dve.wait_ge(carry_done[b], START + i * DC + h)
                        nc.vector.tensor_tensor_scan(scan[:, b, h, :], gate[:, b, h, :], bank[KV[h]][:, :],
                                                     carry[:, b * DC + h:b * DC + h + 1], ALU.mult, ALU.add)\
                            .then_inc(scan_done[b], 1)
                        dve.wait_ge(scan_done[b], START + i * DC + h + 1)
                        nc.vector.tensor_copy(carry[:, b * DC + h:b * DC + h + 1],
                                              scan[:, b, h, BLK - 1:BLK]).then_inc(carry_done[b], 1)
                        dve.wait_ge(q_ready[b], START + i * DC + h + 1)
                        if h == 0:
                            dve.wait_ge(y_transposed[b], START + i)
                        nc.vector.tensor_tensor(y[:, b, h, :], bank[QB][:, :], scan[:, b, h, :],
                                                ALU.mult).then_inc(y_done[b], 1)

                def add_block(b, i):
                    dve.wait_ge(y_transposed[b], START + i + 1)
                    for j in range(2):
                        nc.vector.tensor_tensor(rows(b, i, 2 * j, 2), bank[YB[j]][:, :], rows(b, i, 2 * j, 2),
                                                ALU.add).then_inc(x_added[b], 1)

                def sum_magnitudes():
                    dve.wait_ge(w12_loaded, 32)
                    for n, nat in enumerate((w1_nat, w2_nat)):
                        nc.vector.tensor_reduce(abs_sum[:, n:n + 1], nat[:, :, :], AX.XY, ALU.add,
                                                apply_absolute_value=True).then_inc(abs_done, 1)

                def make_ternary():
                    dve.wait_ge(sum_done, 1)
                    nc.vector.tensor_scalar(thr[:, :], bank[SUMB][:, 0:2], 1.0 / (FF * D), 1e-8, ALU.mult, ALU.max).then_inc(thr_step, 1)
                    dve.wait_ge(thr_step, 1)
                    nc.vector.tensor_scalar(minus_thr[:, :], thr[:, :], -0.5, None, ALU.mult).then_inc(thr_step, 1)
                    dve.wait_ge(thr_step, 2)
                    nc.vector.tensor_scalar(thr[:, :], thr[:, :], 0.5, None, ALU.mult).then_inc(thr_step, 1)
                    dve.wait_ge(thr_step, 3)
                    for n, nat in enumerate((w1_nat, w2_nat)):
                        w = nat[:, :, :].rearrange(flat)
                        if n:
                            dve.wait_ge(tern_done, n)
                        nc.vector.tensor_scalar(below[:, :], w, minus_thr[:, n:n + 1], None, ALU.is_lt).then_inc(below_done, 1)
                        dve.wait_ge(below_done, n + 1)
                        nc.vector.scalar_tensor_tensor(w, w, thr[:, n:n + 1], below[:, :], ALU.is_gt, ALU.subtract)\
                            .then_inc(tern_done, 1)

                def split_vo():
                    for n, (raw, hi, lo) in enumerate(((wv_raw[:, :, :], wv_hi[:, :, :], wv_lo[:, :, :]),
                                                       (wo_raw[:, :], wo_hi[:, :], wo_lo[:, :]))):
                        dve.wait_ge(wvo_high, n + 1)
                        nc.vector.tensor_tensor(lo, raw, hi.bitcast(FP32), ALU.subtract).then_inc(wvo_low, 1)

                def body(i, first, last):
                    for b in range(B):
                        if last:
                            dve.wait_ge(x_added[b], START + 2)
                            ln.dve_statistics(dve, b, 0, NBLK)
                        else:
                            dve.wait_ge(x_loaded[1 if first else 2], 16 * B if first else 16 * B * (NBLK - 2))
                            ln.dve_statistics(dve, b, i + 1, i + 1)
                    for b in range(B):
                        scan_block(b, i)
                        if first and b == 0:
                            sum_magnitudes()
                        if last:
                            dve.wait_ge(ln.rstd_done[b], START + NBLK + 1)
                            ln.dve_normalise(dve, b, 0, NBLK, ln_rstd)
                        else:
                            normalise(b, i + 1)
                    if first:
                        make_ternary()
                    for b in range(B):
                        ln.dve_low(dve, b, i + 1, XB, None if last else gamma_sb)
                    for b in range(B):
                        add_block(b, i)
                    if first:
                        split_vo()

                nc.vector.memset(carry[:, :], 0.0).then_inc(carry_zero, 1)
                dve.wait_ge(carry_zero, 1)
                dve.wait_ge(x_loaded[0], 16 * B)
                for b in range(B):
                    ln.dve_statistics(dve, b, 0, 0)
                for b in range(B):
                    normalise(b, 0)
                for n in range(len(WAB)):
                    dve.wait_ge(wa_high, n + 1)
                    cols = slice(n * BLK, (n + 1) * BLK)
                    nc.vector.tensor_tensor(wa_lo[:, :, :].rearrange(flat)[:, cols], bank[WAB[n]][:, :],
                                            wa_hi[:, :, :].rearrange(flat)[:, cols].bitcast(FP32), ALU.subtract).then_inc(wa_low, 1)
                dve.wait_ge(gamma_loaded, 16)
                for b in range(B):
                    ln.dve_low(dve, b, 0, XB, gamma_sb)
                stage_loop(dve, body)

        wqa.close()

        def feed_forward(tag, stage, w1t, w2t, final):
            with ExitStack() as st:
                sem, sems = semaphores(st)
                hidden = sbuf(st, f"{tag}_hidden", [P, 4, BLK])
                hid_hi = sbuf(st, f"{tag}_hid_hi", [P, B, FC, BLK], FP32R)
                hid_lo = sbuf(st, f"{tag}_hid_lo", [P, B, FC, BLK], FP32R)
                h_ready, gelu_done, hhigh_done, hlow_done = sem(f"{tag}_h"), sem(f"{tag}_gelu"), sem(f"{tag}_hhigh"), sem(f"{tag}_hlow")
                out_ready, x_added, b2_added = sems(f"{tag}_out"), sems(f"{tag}_xadd"), sems(f"{tag}_b2")
                stored, w_loaded, w_saved = sem(f"{tag}_store"), sem(f"{tag}_wload"), sem(f"{tag}_wsave")
                n0 = stage * NBLK
                XB, HB, OB = (0, 1), (2, 3), ((4, 5), (6, 7))
                block = st.enter_context(nc.Block())

                @block.sync
                def _(sp):
                    if not final:
                        sp.dma_start(w1t_dram, w1t[:, :, :].rearrange("p a b -> p (a b)").bitcast(FP32)).then_inc(w_saved, 16)
                        sp.dma_start(w2t_dram, w2t[:, :, :].rearrange("p a b -> p (a b)").bitcast(FP32)).then_inc(w_saved, 16)
                        sp.wait_ge(w_saved, 32)
                    if final:
                        sp.dma_start(w1t[:, :, :].rearrange("p a b -> p (a b)").bitcast(FP32), w1t_dram).then_inc(w_loaded, 16)
                        sp.dma_start(w2t[:, :, :].rearrange("p a b -> p (a b)").bitcast(FP32), w2t_dram).then_inc(w_loaded, 16)
                        with sp.Fori(0, NBLK) as i:
                            for b in range(B):
                                sp.wait_ge(x_added[b], START + (i + 1) * 2)
                                sp.dma_start(out_view[b, :, bass.ds(i * CH, CH), :],
                                             rows(b, i, 0, CH).rearrange("p (n d) -> p n d", d=D)).then_inc(stored, 16)
                        sp.wait_ge(stored, 16 * B * NBLK)

                @block.gpsimd
                def _(pool):
                    start_counts(pool, b2_added)
                    def body(i, more):
                        if more or not final:
                            for b in range(B):
                                ln.pool_rstd(pool, b, n0 + i + 1)
                        for b in range(B):
                            pool.wait_ge(ln.normalised[b], START + (n0 + i + 1) * CH)
                            nc.gpsimd.tensor_tensor(rows(b, i, 0, CH).rearrange("p (n d) -> p n d", d=D),
                                                    rows(b, i, 0, CH).rearrange("p (n d) -> p n d", d=D),
                                                    b2_sb[:, None, :].to_broadcast([P, CH, D]),
                                                    ALU.add).then_inc(b2_added[b], 1)
                    with pool.Fori(0, NBLK - 1) as i:
                        body(i, True)
                    body(NBLK - 1, False)

                @block.tensor
                def _(pe):
                    start_counts(pe, h_ready, out_ready)
                    def up(b, i):
                        pe.wait_ge(ln.low_done[b], START + (n0 + i + 1) * DC)
                        for f in range(FC):
                            pe.wait_ge(gelu_done, START + i * (2 * FC) + max(b * FC + f - 1, 0))
                            for k in range(DC):
                                w = w1t[:, k, f * P:(f + 1) * P]
                                nc.tensor.matmul(bank[HB[f % 2]][:, :], w, ln.xhi[:, b, k, :], start=(k == 0), stop=False)
                                last = nc.tensor.matmul(bank[HB[f % 2]][:, :], w, ln.xlo[:, b, k, :],
                                                        start=False, stop=(k == DC - 1))
                            last.then_inc(h_ready, 1)

                    def down(b, i):
                        pe.wait_ge(hlow_done, START + i * (2 * FC) + (b + 1) * FC)
                        pe.wait_ge(x_added[b], START + i * 2)
                        for c in range(CH):
                            dst = bank[OB[b][c // 2]][:, (c % 2) * D:(c % 2 + 1) * D]
                            for f in range(FC):
                                nc.tensor.matmul(dst, hid_hi[:, b, f, c * P:(c + 1) * P], w2t[:, f, :],
                                                 start=(f == 0), stop=False)
                                last = nc.tensor.matmul(dst, hid_lo[:, b, f, c * P:(c + 1) * P], w2t[:, f, :],
                                                        start=False, stop=(f == FC - 1))
                            if c % 2:
                                last.then_inc(out_ready[b], 1)

                    def prepare(b, n):
                        if b:
                            pe.wait_ge(ln.low_done[0], START + (n + 1) * DC)
                        else:
                            pe.wait_ge(ln.low_done[1], START + n * DC)
                        ln.pe_transpose(pe, b, n, XB)

                    def body(i, more):
                        for b in range(B):
                            up(b, i)
                        if more or not final:
                            for b in range(B):
                                prepare(b, n0 + i + 1)
                        for b in range(B):
                            down(b, i)

                    if final:
                        pe.wait_ge(w_loaded, 32)
                    with pe.Fori(0, NBLK - 1) as i:
                        body(i, True)
                    body(NBLK - 1, False)

                @block.scalar
                def _(act):
                    start_counts(act, gelu_done, hhigh_done)
                    def high(b, i, f):
                        act.wait_ge(gelu_done, START + i * (2 * FC) + b * FC + f + 1)
                        nc.scalar.copy(hid_hi[:, b, f, :], hidden[:, f % 4, :]).then_inc(hhigh_done, 1)

                    def body(i, more):
                        for b in range(B):
                            act.wait_ge(out_ready[b], START + i * 2)
                            for f in range(FC):
                                act.wait_ge(h_ready, START + i * (2 * FC) + b * FC + f + 1)
                                act.wait_ge(hlow_done, START + i * (2 * FC) + max(b * FC + f - 3, 0))
                                nc.scalar.activation(hidden[:, f % 4, :], bank[HB[f % 2]][:, :], ACT.Gelu,
                                                     bias=b1_sb[:, f:f + 1]).then_inc(gelu_done, 1)
                                if f:
                                    high(b, i, f - 1)
                            high(b, i, FC - 1)
                        if more or not final:
                            for b in range(B):
                                ln.act_high(act, b, n0 + i + 1, XB)

                    with act.Fori(0, NBLK - 1) as i:
                        body(i, True)
                    body(NBLK - 1, False)

                @block.vector
                def _(dve):
                    start_counts(dve, hlow_done, x_added)
                    def body(i, more):
                        for b in range(B):
                            dve.wait_ge(out_ready[b], START + i * 2)
                            for f in range(FC):
                                dve.wait_ge(hhigh_done, START + i * (2 * FC) + b * FC + f + 1)
                                nc.vector.tensor_tensor(hid_lo[:, b, f, :], hidden[:, f % 4, :],
                                                        hid_hi[:, b, f, :].bitcast(FP32), ALU.subtract).then_inc(hlow_done, 1)
                                after = i + 1 if more else 0
                                if (more or not final) and f == 1:
                                    if not more:
                                        dve.wait_ge(x_added[b], START + 2)
                                    ln.dve_statistics(dve, b, after, n0 + i + 1)
                                if (more or not final) and f == 5:
                                    dve.wait_ge(ln.rstd_done[b], START + n0 + i + 2)
                                    ln.dve_normalise(dve, b, after, n0 + i + 1, ln_rstd)
                        if more or not final:
                            for b in range(B):
                                ln.dve_low(dve, b, n0 + i + 1, XB)
                        for b in range(B):
                            dve.wait_ge(b2_added[b], START + i + 1)
                            for j in range(2):
                                dve.wait_ge(out_ready[b], START + i * 2 + j + 1)
                                nc.vector.tensor_tensor(rows(b, i, 2 * j, 2), bank[OB[b][j]][:, :], rows(b, i, 2 * j, 2),
                                                        ALU.add).then_inc(x_added[b], 1)

                    with dve.Fori(0, NBLK - 1) as i:
                        body(i, True)
                    body(NBLK - 1, False)

        feed_forward("B", 1, w1t, w2t, False)
        tern.close()

        with ExitStack() as st:
            sem, sems = semaphores(st)
            causal = sbuf(st, "causal", [P, CH, P])
            own_head = sbuf(st, "own_head", [P, CH, P])
            v_all = sbuf(st, "v_all", [P, B, CH, H * DK])
            w_raw = sbuf(st, "w_raw", [P, 2, DC, P])
            w_hi = sbuf(st, "w_hi", [P, 2, DC, P], FP32R)
            w_lo = sbuf(st, "w_lo", [P, 2, DC, P], FP32R)
            qt = sbuf(st, "qt", [P, B, BLK])
            kt = sbuf(st, "kt", [P, B, BLK])
            krow = sbuf(st, "krow", [P, B, CH, P])
            vrow = sbuf(st, "vrow", [P, B, CH, P])
            scores = sbuf(st, "scores", [P, B, 2, CH, P])
            ut = sbuf(st, "ut", [P, B, BLK])
            urow = sbuf(st, "urow", [P, B, CH, P])
            ot_hi = sbuf(st, "ot_hi", [P, B, BLK], FP32R)
            ot_lo = sbuf(st, "ot_lo", [P, B, BLK], FP32R)
            s_state = sbuf(st, "s_state", [P, B, CH + 1, P])
            p_state = sbuf(st, "p_state", [P, B, CH + 1, P])
            s_carry = sbuf(st, "s_carry", [P, B * PAIRS * P])
            p_carry = sbuf(st, "p_carry", [P, B * PAIRS * P])

            w_loaded, w_high, w_low = sem("C_wload"), sem("C_whigh"), sem("C_wlow")
            mask_zero, masks_done, carry_zero = sem("C_maskzero"), sem("C_masks"), sem("C_zero")
            v_ready, v_stored = sem("C_v"), sem("C_vstore")
            q_ready, k_ready, qt_done, kt_done = sems("C_q"), sems("C_k"), sems("C_qt"), sems("C_kt")
            krow_ready, krow_done = sems("C_krp"), sems("C_krow")
            a_ready, a_masked, b_ready, b_masked = sems("C_a"), sems("C_am"), sems("C_b"), sems("C_bm")
            s_ready, s_masked, s_summed = sems("C_s"), sems("C_sm"), sems("C_ss")
            p_ready, p_masked, p_summed = sems("C_p"), sems("C_pm"), sems("C_ps")
            ut_ready, ut_done, urow_ready, urow_done = sems("C_utp"), sems("C_ut"), sems("C_urp"), sems("C_urow")
            o_ready, o_high, o_low = sems("C_o"), sems("C_oh"), sems("C_ol")
            out_ready, x_added = sems("C_out"), sems("C_xadd")
            s_carried, p_carried, vrow_done = sems("C_sc"), sems("C_pc"), sems("C_vr")

            QB, KB, AB = (0, 2), (1, 3), ((0, 1), (2, 3))
            KRB, UB, URB, PB = (4, 5), (4, 5), (4, 5), (4, 5)
            SB, OB, YB = (6, 7), (6, 7), ((4, 5), (6, 7))
            XB = ((0, 1), (2, 3))
            VB = (4, 5, 6, 7)
            V_OUT = B * CH * 2
            n0 = 2 * NBLK
            block = st.enter_context(nc.Block())

            def unit_loops(eng, block_start, unit):
                def one_block(i, last):
                    block_start(i)
                    with eng.Fori(0, PAIRS - 1) as p:
                        unit(i, p, i * PAIRS + p, False, False)
                    unit(i, PAIRS - 1, i * PAIRS + (PAIRS - 1), True, last)
                with eng.Fori(0, NBLK - 1) as i:
                    one_block(i, False)
                one_block(NBLK - 1, True)

            @block.sync
            def _(sp):
                start_counts(sp, w_loaded)
                with sp.Fori(0, NBLK) as i:
                    with sp.Fori(0, PAIRS) as p:
                        sp.wait_ge(w_low, START + i * PAIRS + p)
                        sp.dma_start(w_raw[:, 0:1, :, :],
                                     wq_view[:, bass.ds(p, 1)]).then_inc(w_loaded, 16)
                        sp.dma_start(w_raw[:, 1:2, :, :],
                                     wk_view[:, bass.ds(p, 1)]).then_inc(w_loaded, 16)

            @block.gpsimd
            def _(pool):
                nc.gpsimd.memset(causal[:, :, :], 1.0).then_inc(mask_zero, 1)
                nc.gpsimd.memset(own_head[:, :, :], 1.0).then_inc(mask_zero, 1)
                pool.wait_ge(mask_zero, 2)
                nc.gpsimd.affine_select(out=causal[:, :, :], in_=causal[:, :, :], compare_op=ALU.is_ge, fill=0.0,
                                        base=0, pattern=[[0, CH], [1, P]], channel_multiplier=-1).then_inc(masks_done, 1)
                for h, base, step in ((0, DK - 1, -1), (1, -DK, 1)):
                    part = own_head[:, :, h * DK:(h + 1) * DK]
                    nc.gpsimd.affine_select(out=part, in_=part, compare_op=ALU.is_ge, fill=0.0, base=base,
                                            pattern=[[0, CH], [0, DK]], channel_multiplier=step).then_inc(masks_done, 1)

                with pool.Fori(1, NBLK + 1) as i:
                    for b in range(B):
                        ln.pool_rstd(pool, b, n0 + i)

            @block.tensor
            def _(pe):
                start_counts(pe, v_ready, q_ready, k_ready, krow_ready, a_ready, b_ready,
                             s_ready, p_ready, ut_ready, urow_ready, o_ready, out_ready)
                def block_start(i):
                    for b in range(B):
                        pe.wait_ge(ln.low_done[b], START + (n0 + i + 1) * DC)
                        for c in range(CH):
                            for half in range(2):
                                n = (b * CH + c) * 2 + half
                                if n < len(VB):
                                    pe.wait_ge(x_added[n // 2], START + i * PAIRS * 2)
                                else:
                                    pe.wait_ge(v_stored, START + i * V_OUT + n - len(VB) + 1)
                                dst = bank[VB[n % len(VB)]][:, :]
                                for k in range(DC):
                                    x_hi, x_lo = ln.xhi[:, b, k, c * P:(c + 1) * P], ln.xlo[:, b, k, c * P:(c + 1) * P]
                                    cols = slice(half * BLK, (half + 1) * BLK)
                                    nc.tensor.matmul(dst, x_hi, wv_hi[:, k, cols], start=(k == 0), stop=False)
                                    nc.tensor.matmul(dst, x_hi, wv_lo[:, k, cols], start=False, stop=False)
                                    last = nc.tensor.matmul(dst, x_lo, wv_hi[:, k, cols], start=False, stop=(k == DC - 1))
                                last.then_inc(v_ready, 1)
                    for b in range(B):
                        project(b, i * PAIRS)

                def project(b, u):
                    pe.wait_ge(w_low, START + u + 1)
                    for part, dst, ready in ((0, QB[b], q_ready), (1, KB[b], k_ready)):
                        for k in range(DC):
                            last = pe_split_product(bank[dst][:, :], w_hi[:, part, k, :], w_lo[:, part, k, :],
                                                    ln.xhi[:, b, k, :], ln.xlo[:, b, k, :], k, DC - 1)
                        last.then_inc(ready[b], 1)

                def scores_of(keys, b, ready):
                    for h in range(2):
                        hd = slice(h * DK, (h + 1) * DK)
                        for c in range(CH):
                            tok = slice(c * P, (c + 1) * P)
                            last = nc.tensor.matmul(bank[AB[b][h]][:, tok], keys[hd, b, tok], qt[hd, b, tok], start=True, stop=True)
                        last.then_inc(ready[b], 1)

                def by_scores(row, dst, b):
                    for c in range(CH):
                        tok = slice(c * P, (c + 1) * P)
                        for h in range(2):
                            hd = slice(h * DK, (h + 1) * DK)
                            nc.tensor.matmul(bank[dst[b]][hd, tok], row[:, b, c, hd], scores[:, b, h, c, :],
                                             start=(c == 0), stop=False, skip_group_check=True)

                def by_state(pe, state, dst, b, u, summed):
                    for c in range(CH):
                        tok = slice(c * P, (c + 1) * P)
                        if c:
                            pe.wait_ge(summed[b], START + u * CH + c)
                        last = nc.tensor.matmul(bank[dst[b]][:, tok], state[:, b, c, :], qt[:, b, tok],
                                                start=False, stop=(c == CH - 1), skip_group_check=True)
                    return last

                def unit(i, p, u, block_end, end):
                    pe.wait_ge(v_stored, START + (i + 1) * V_OUT)
                    for b in range(B):
                        pe.wait_ge(kt_done[b], START + u + 1)
                        pe.wait_ge(x_added[0], START + u * 2)
                        for c in range(CH):
                            tok = slice(c * P, (c + 1) * P)
                            last = nc.tensor.transpose(bank[KRB[b]][:, tok], kt[:, b, tok], ident[:, :])
                        last.then_inc(krow_ready[b], 1)
                    for b in range(B):
                        pe.wait_ge(qt_done[b], START + u + 1)
                        scores_of(kt, b, a_ready)
                        pe.wait_ge(krow_done[b], START + u + 1)
                        pe.wait_ge(x_added[1], START + u * 2)
                        for c in range(CH):
                            last = nc.tensor.matmul(bank[SB[b]][:, c * P:(c + 1) * P], krow[:, b, c, :], krow[:, b, c, :],
                                                    start=True, stop=True)
                        last.then_inc(s_ready[b], 1)
                    for b in range(B):
                        pe.wait_ge(a_masked[b], START + (u + 1) * 2)
                        by_scores(krow, UB, b)
                        pe.wait_ge(s_carried[b], START + u + 1)
                        by_state(pe, s_state, UB, b, u, s_summed).then_inc(ut_ready[b], 1)
                    for b in range(B):
                        pe.wait_ge(ut_done[b], START + u + 1)
                        scores_of(ut, b, b_ready)
                    for b in range(B):
                        for c in range(CH):
                            tok = slice(c * P, (c + 1) * P)
                            last = nc.tensor.transpose(bank[URB[b]][:, tok], ut[:, b, tok], ident[:, :])
                        last.then_inc(urow_ready[b], 1)
                    for b in range(B):
                        pe.wait_ge(b_masked[b], START + (u + 1) * 2)
                        pe.wait_ge(vrow_done[b], START + u + 1)
                        pe.wait_ge(s_masked[b], START + u + 1)
                        by_scores(vrow, OB, b)
                        pe.wait_ge(urow_done[b], START + u + 1)
                        for c in range(CH):
                            last = nc.tensor.matmul(bank[PB[b]][:, c * P:(c + 1) * P], urow[:, b, c, :], vrow[:, b, c, :],
                                                    start=True, stop=True)
                        last.then_inc(p_ready[b], 1)
                    for b in range(B):
                        pe.wait_ge(p_carried[b], START + u + 1)
                        by_state(pe, p_state, OB, b, u, p_summed).then_inc(o_ready[b], 1)
                        if not block_end:
                            project(b, u + 1)
                    for b in range(B):
                        if block_end:
                            ln.pe_transpose(pe, b, n0 + i + 1, XB[b])
                        pe.wait_ge(o_low[b], START + u + 1)
                        if b:
                            pe.wait_ge(o_low[0], START + u + 1)
                        else:
                            pe.wait_ge(p_masked[1], START + u + 1)
                        for c in range(CH):
                            tok = slice(c * P, (c + 1) * P)
                            dst = bank[YB[b][c // 2]][:, (c % 2) * D:(c % 2 + 1) * D]
                            w = [x[:, bass.ds(p * D, D)] for x in (wo_hi, wo_lo)]
                            nc.tensor.matmul(dst, ot_hi[:, b, tok], w[0], start=True, stop=False)
                            nc.tensor.matmul(dst, ot_hi[:, b, tok], w[1], start=False, stop=False)
                            last = nc.tensor.matmul(dst, ot_lo[:, b, tok], w[0], start=False, stop=True)
                            if c % 2:
                                last.then_inc(out_ready[b], 1)

                unit_loops(pe, block_start, unit)

            @block.scalar
            def _(act):
                start_counts(act, w_high, v_stored, qt_done, kt_done, krow_done, ut_done,
                             urow_done, o_high)
                def split_weights(u):
                    act.wait_ge(w_loaded, START + (u + 1) * 32)
                    act.wait_ge(k_ready[1], START + u)
                    nc.scalar.copy(w_hi[:, :, :, :], w_raw[:, :, :, :]).then_inc(w_high, 1)

                def block_start(i):
                    act.wait_ge(vrow_done[1], START + i * PAIRS)
                    for n in range(V_OUT):
                        act.wait_ge(v_ready, START + i * V_OUT + n + 1)
                        b, c, half = n // (2 * CH), n // 2 % CH, n % 2
                        nc.scalar.copy(v_all[:, b, c, half * BLK:(half + 1) * BLK], bank[VB[n % len(VB)]][:, :])\
                            .then_inc(v_stored, 1)

                    for b in range(B):
                        store_qk(b, i * PAIRS)

                def store_qk(b, u):
                    act.wait_ge(q_ready[b], START + u + 1)
                    act.wait_ge(o_ready[b], START + u)
                    nc.scalar.copy(qt[:, b, :], bank[QB[b]][:, :]).then_inc(qt_done[b], 1)
                    act.wait_ge(k_ready[b], START + u + 1)
                    act.wait_ge(a_ready[b], START + u * 2)
                    nc.scalar.copy(kt[:, b, :], bank[KB[b]][:, :]).then_inc(kt_done[b], 1)

                def unit(i, p, u, block_end, end):
                    for b in range(B):
                        act.wait_ge(krow_ready[b], START + u + 1)
                        act.wait_ge(ut_ready[b], START + u)
                        nc.scalar.copy(krow[:, b, :, :].rearrange("p c d -> p (c d)"), bank[KRB[b]][:, :]).then_inc(krow_done[b], 1)
                    if not end:
                        split_weights(u + 1)
                    for b in range(B):
                        act.wait_ge(ut_ready[b], START + u + 1)
                        nc.scalar.copy(ut[:, b, :], bank[UB[b]][:, :]).then_inc(ut_done[b], 1)
                    for b in range(B):
                        act.wait_ge(urow_ready[b], START + u + 1)
                        act.wait_ge(p_ready[b], START + u)
                        nc.scalar.copy(urow[:, b, :, :].rearrange("p c d -> p (c d)"), bank[URB[b]][:, :]).then_inc(urow_done[b], 1)
                    for b in range(B):
                        act.wait_ge(o_ready[b], START + u + 1)
                        act.wait_ge(out_ready[b], START + u * 2)
                        nc.scalar.copy(ot_hi[:, b, :], bank[OB[b]][:, :]).then_inc(o_high[b], 1)
                        if not block_end:
                            store_qk(b, u + 1)
                    if block_end:
                        for b in range(B):
                            ln.act_high(act, b, n0 + i + 1, XB[b])

                split_weights(0)
                unit_loops(act, block_start, unit)

            @block.vector
            def _(dve):
                start_counts(dve, w_low, a_masked, b_masked,
                             s_masked, s_summed, s_carried, p_masked, p_summed, p_carried, vrow_done, o_low, x_added)
                def split_weights(u):
                    dve.wait_ge(w_high, START + u + 1)
                    nc.vector.tensor_tensor(w_lo[:, :, :, :], w_raw[:, :, :, :], w_hi[:, :, :, :].bitcast(FP32),
                                            ALU.subtract).then_inc(w_low, 1)

                def mask_scores(b, u, ready, masked):
                    for h in range(2):
                        dve.wait_ge(ready[b], START + u * 2 + h + 1)
                        nc.vector.tensor_tensor(scores[:, b, h, :, :], bank[AB[b][h]][:, :].rearrange("p (c d) -> p c d", c=CH),
                                                causal[:, :, :], ALU.mult).then_inc(masked[b], 1)

                def sum_states(b, p, u, SBANK, state, carry, ready, masked, summed, carried):
                    dve.wait_ge(ready[b], START + u + 1)
                    nc.vector.tensor_tensor(state[:, b, 1:, :], bank[SBANK[b]][:, :].rearrange("p (c d) -> p c d", c=CH),
                                            own_head[:, :, :], ALU.mult).then_inc(masked[b], 1)
                    dve.wait_ge(masked[b], START + u + 1)
                    dve.wait_ge(carried[b], START + u + 1)
                    for c in range(CH):
                        if c:
                            dve.wait_ge(summed[b], START + u * CH + c)
                        dst = state[:, b, c + 1, :] if c < CH - 1 else carry[:, bass.ds((p + b * PAIRS) * P, P)]
                        nc.vector.tensor_tensor(dst, state[:, b, c + 1, :], state[:, b, c, :], ALU.add).then_inc(summed[b], 1)

                def block_start(i):
                    pass

                def unit(i, p, u, block_end, end):
                    for b in range(B):
                        dve.wait_ge(s_summed[b], START + u * CH)
                        dve.wait_ge(ut_ready[b], START + u)
                        nc.vector.tensor_copy(s_state[:, b, 0, :], s_carry[:, bass.ds((p + b * PAIRS) * P, P)])\
                            .then_inc(s_carried[b], 1)
                        dve.wait_ge(p_summed[b], START + u * CH)
                        dve.wait_ge(o_ready[b], START + u)
                        nc.vector.tensor_copy(p_state[:, b, 0, :], p_carry[:, bass.ds((p + b * PAIRS) * P, P)])\
                            .then_inc(p_carried[b], 1)
                        dve.wait_ge(v_stored, START + (i + 1) * V_OUT)
                        nc.vector.tensor_copy(vrow[:, b, :, :], v_all[:, b, :, bass.ds(p * P, P)]).then_inc(vrow_done[b], 1)
                    for b in range(B):
                        mask_scores(b, u, a_ready, a_masked)
                        sum_states(b, p, u, SB, s_state, s_carry, s_ready, s_masked, s_summed, s_carried)
                    if not end:
                        split_weights(u + 1)
                    after = 0 if end else i + 1
                    if block_end:
                        for b in range(B):
                            if end:
                                dve.wait_ge(x_added[b], START + PAIRS * 2)
                            ln.dve_statistics(dve, b, after, n0 + i + 1)
                    for b in range(B):
                        dve.wait_ge(ut_ready[b], START + u + 1)
                        mask_scores(b, u, b_ready, b_masked)
                    for b in range(B):
                        sum_states(b, p, u, PB, p_state, p_carry, p_ready, p_masked, p_summed, p_carried)
                    if block_end:
                        for b in range(B):
                            dve.wait_ge(ln.rstd_done[b], START + n0 + i + 2)
                            ln.dve_normalise(dve, b, after, n0 + i + 1, ln_rstd)
                    for b in range(B):
                        dve.wait_ge(o_high[b], START + u + 1)
                        nc.vector.tensor_tensor(ot_lo[:, b, :], bank[OB[b]][:, :], ot_hi[:, b, :].bitcast(FP32),
                                                ALU.subtract).then_inc(o_low[b], 1)
                    for b in range(B):
                        if block_end:
                            ln.dve_low(dve, b, n0 + i + 1, XB[b])
                        for j in range(2):
                            dve.wait_ge(out_ready[b], START + u * 2 + j + 1)
                            nc.vector.tensor_tensor(rows(b, i, 2 * j, 2), bank[YB[b][j]][:, :], rows(b, i, 2 * j, 2),
                                                    ALU.add).then_inc(x_added[b], 1)

                nc.vector.memset(s_carry[:, :], 0.0).then_inc(carry_zero, 1)
                nc.vector.memset(p_carry[:, :], 0.0).then_inc(carry_zero, 1)
                split_weights(0)
                dve.wait_ge(carry_zero, 2)
                dve.wait_ge(masks_done, 3)
                unit_loops(dve, block_start, unit)

        with ExitStack() as st:
            w1t = sbuf(st, "w1t_d", [P, DC, FF], FP32R)
            w2t = sbuf(st, "w2t_d", [P, FC, D], FP32R)
            feed_forward("D", 3, w1t, w2t, True)


_INS = ["L0_attn_a_x", "L0_attn_a_gamma", "L0_attn_a_w_qkva", "L0_attn_b_W_q", "L0_attn_b_W_k", "L0_attn_b_W_v",
        "L0_attn_b_W_o", "L0_ffn_W1", "L0_ffn_b1", "L0_ffn_W2", "L0_ffn_b2"]
_OUTS = [((B, T, D), "float32")]


def kernel(**inputs):
    import numpy as _np
    import concourse.bacc as _bacc
    from concourse import mybir as _mybir
    from concourse.bass_utils import run_bass_kernel_spmd as _run

    nc = _bacc.Bacc("TRN2", target_bir_lowering=False, num_devices=1)
    arrays, args = {}, []
    for name in _INS:
        a = _np.ascontiguousarray(inputs[name])
        arrays[f"in_{name}_dram"] = a
        args.append(nc.dram_tensor(f"in_{name}_dram", a.shape, _mybir.dt.from_np(a.dtype), kind="ExternalInput").ap())
    for i, (shape, dtype) in enumerate(_OUTS):
        dt = _mybir.dt.from_np(_np.dtype(dtype))
        args.append(nc.dram_tensor(f"out_{i}_dram", shape, dt, kind="ExternalOutput").ap())
    hybrid_kernel(nc, *args)
    r = _run(nc, [arrays], core_ids=[0])
    got = tuple(r.results[0][f"out_{i}_dram"] for i in range(len(_OUTS)))
    return got[0]
```

```python
import concourse.bass as bass
from concourse import mybir
from contextlib import ExitStack

FP32 = mybir.dt.float32
FP32R = mybir.dt.float32r
ALU = mybir.AluOpType
ACT = mybir.ActivationFunctionType

START = 1

P = 128
B, T, D = 2, 2048, 256
DC = D // P
BLK = 512
CH = BLK // P
NBLK = T // BLK
TILES = T // P
FF = 1024
FC = FF // P
H, DK = 16, 64
PAIRS = H // 2
QKVA = 3 * D
LN_EPS = 1e-5
RMS_EPS = 1e-12


def hybrid_kernel(nc, x_d, gamma_d, wqkva_d, wq_d, wk_d, wv_d, wo_d, w1_d, b1_d, w2_d, b2_d, out_d):
    x_view = x_d.rearrange("b (n p) d -> b p n d", p=P)
    out_view = out_d.rearrange("b (n p) d -> b p n d", p=P)
    wq_view = wq_d.rearrange("(k p) (n c) -> p n k c", p=P, c=P)
    wk_view = wk_d.rearrange("(k p) (n c) -> p n k c", p=P, c=P)

    outer = ExitStack()
    with outer:
        def sbuf(stack, name, shape, dtype=FP32):
            return stack.enter_context(nc.sbuf_tensor(name, shape, dtype))

        def semaphores(stack):
            used = []

            @stack.callback
            def _():
                with nc.Block() as block:
                    @block.gpsimd
                    def _(pool):
                        nums = sorted(s.num for s in used)
                        starts = [n for n in nums if n - 1 not in nums]
                        ends = [n + 1 for n in nums if n + 1 not in nums]
                        for first, end in zip(starts, ends):
                            pool.sem_clear(range(first, end))
                for s in used:
                    nc.release_semaphore(s)

            def sem(name):
                used.append(nc.alloc_semaphore(name))
                return used[-1]

            def sems(name):
                return [sem(f"{name}{b}") for b in range(B)]
            return sem, sems

        xres = sbuf(outer, "xres", [P, B * TILES * D])
        ident = sbuf(outer, "ident", [P, P])
        wv_hi = sbuf(outer, "wv_hi", [P, DC, H * DK], FP32R)
        wv_lo = sbuf(outer, "wv_lo", [P, DC, H * DK], FP32R)
        wo_hi = sbuf(outer, "wo_hi", [P, PAIRS * D], FP32R)
        wo_lo = sbuf(outer, "wo_lo", [P, PAIRS * D], FP32R)
        b1_sb = sbuf(outer, "b1_sb", [P, FC])
        b2_sb = sbuf(outer, "b2_sb", [P, D])
        gamma_sb = sbuf(outer, "gamma_sb", [P, DC])
        ln_stats = sbuf(outer, "ln_stats", [P, B, CH, 6])
        ln_moments = sbuf(outer, "ln_moments", [P, B, CH, 2])
        ln_vare = sbuf(outer, "ln_vare", [P, B, CH])
        ln_rstd = sbuf(outer, "ln_rstd", [P, B, CH])
        ln_filler = sbuf(outer, "ln_filler", [P, 1])
        ln_eps = sbuf(outer, "ln_eps", [P, CH])
        minus_half = sbuf(outer, "minus_half", [P, CH])
        plus_half = sbuf(outer, "plus_half", [P, CH])
        bank = [outer.enter_context(nc.psum_tensor(f"bank{i}", [P, BLK], FP32)) for i in range(8)]
        w1t_dram = nc.dram_tensor("w1t_scratch", (P, DC * FF), FP32, kind="Internal").ap()
        w2t_dram = nc.dram_tensor("w2t_scratch", (P, FC * D), FP32, kind="Internal").ap()

        def start_counts(eng, *semaphores_of_eng):
            for s in semaphores_of_eng:
                for one in (s if isinstance(s, list) else [s]):
                    eng.sem_inc(one, START)

        def rows(b, i, c=0, n=1):
            return xres[:, bass.ds((i * CH + (b * TILES + c)) * D, n * D)]

        class LayerNorm:
            def __init__(self, stack, sems):
                self.xn = sbuf(stack, "ln_xn", [P, B, CH, D])
                self.xhi = sbuf(stack, "ln_xhi", [P, B, DC, BLK], FP32R)
                self.xlo = sbuf(stack, "ln_xlo", [P, B, DC, BLK], FP32R)
                self.stats_done = sems("ln_stats_done")
                self.moments_done = sems("ln_moments_done")
                self.vare_done = sems("ln_vare_done")
                self.rstd_done = sems("ln_rstd_done")
                self.normalised = sems("ln_normalised")
                self.transposed = sems("ln_transposed")
                self.high_done = sems("ln_high_done")
                self.low_done = sems("ln_low_done")

            def dve_statistics(self, dve, b, i, n):
                for c in range(CH):
                    nc.vector.bn_stats(ln_stats[:, b, c, :], rows(b, i, c)).then_inc(self.stats_done[b], 1)
                dve.wait_ge(self.stats_done[b], START + (n + 1) * CH)
                nc.vector.memset(ln_filler[:, :], 0.0)
                for c in range(CH):
                    nc.vector.bn_aggr(ln_moments[:, b, c, :], ln_stats[:, b, c, :]).then_inc(self.moments_done[b], 1)

            def pool_rstd(self, pool, b, n):
                pool.wait_ge(self.moments_done[b], START + (n + 1) * CH)
                nc.gpsimd.tensor_tensor(ln_vare[:, b, :], ln_moments[:, b, :, 1], ln_eps[:, :],
                                        ALU.add).then_inc(self.vare_done[b], 1)
                pool.wait_ge(self.vare_done[b], START + n + 1)
                nc.gpsimd.tensor_tensor(ln_rstd[:, b, :], ln_vare[:, b, :], minus_half[:, :],
                                        ALU.pow).then_inc(self.rstd_done[b], 1)

            def dve_normalise(self, dve, b, i, n, factor):
                dve.wait_ge(self.transposed[b], START + n * DC)
                for c in range(CH):
                    nc.vector.tensor_scalar(self.xn[:, b, c, :], rows(b, i, c), ln_moments[:, b, c, 0:1],
                                            factor[:, b, c:c + 1], ALU.subtract, ALU.mult)\
                        .then_inc(self.normalised[b], 1)

            def pe_transpose(self, pe, b, n, banks):
                pe.wait_ge(self.normalised[b], START + (n + 1) * CH)
                for k in range(DC):
                    for c in range(CH):
                        last = nc.tensor.transpose(bank[banks[k]][:, c * P:(c + 1) * P],
                                                   self.xn[:, b, c, k * P:(k + 1) * P], ident[:, :])
                    last.then_inc(self.transposed[b], 1)

            def act_high(self, act, b, n, banks, scale=None):
                for k in range(DC):
                    act.wait_ge(self.transposed[b], START + n * DC + k + 1)
                    nc.scalar.activation(self.xhi[:, b, k, :], bank[banks[k]][:, :], ACT.Identity,
                                         scale=1.0 if scale is None else scale[:, k:k + 1])\
                        .then_inc(self.high_done[b], 1)

            def dve_low(self, dve, b, n, banks, scale=None):
                for k in range(DC):
                    dve.wait_ge(self.high_done[b], START + n * DC + k + 1)
                    if scale is None:
                        nc.vector.tensor_tensor(self.xlo[:, b, k, :], bank[banks[k]][:, :],
                                                self.xhi[:, b, k, :].bitcast(FP32), ALU.subtract)\
                            .then_inc(self.low_done[b], 1)
                    else:
                        nc.vector.scalar_tensor_tensor(self.xlo[:, b, k, :], bank[banks[k]][:, :],
                                                       scale[:, k:k + 1], self.xhi[:, b, k, :].bitcast(FP32),
                                                       ALU.mult, ALU.subtract).then_inc(self.low_done[b], 1)

        w1t_again = wv_hi[:, :, :]
        w2t_again = wv_lo[:, :, :].rearrange("p a b -> p (a b)").rearrange("p (f d) -> p f d", d=D)

        ln = LayerNorm(outer, semaphores(outer)[1])

        def pe_split_product(out, w_hi, w_lo, x_hi, x_lo, k, last_k):
            nc.tensor.matmul(out, w_hi, x_hi, start=(k == 0), stop=False)
            nc.tensor.matmul(out, w_hi, x_lo, start=False, stop=False)
            return nc.tensor.matmul(out, w_lo, x_hi, start=False, stop=(k == last_k))

        tern = outer.enter_context(ExitStack())
        w1t = sbuf(tern, "w1t", [P, DC, FF], FP32R)
        w2t = sbuf(tern, "w2t", [P, FC, D], FP32R)
        wqa = tern.enter_context(ExitStack())
        wa_hi = sbuf(wqa, "wa_hi", [P, DC, QKVA], FP32R)
        wa_lo = sbuf(wqa, "wa_lo", [P, DC, QKVA], FP32R)

        with ExitStack() as st:
            sem, sems = semaphores(st)
            wa_nat = sbuf(st, "wa_nat", [P, QKVA // P, D])
            w1_nat = sbuf(st, "w1_nat", [P, FC, D])
            w2_nat = sbuf(st, "w2_nat", [P, DC, FF])
            below = sbuf(st, "below", [P, FC * D])
            wv_raw = sbuf(st, "wv_raw", [P, DC, H * DK])
            wo_raw = sbuf(st, "wo_raw", [P, PAIRS * D])
            ones = sbuf(st, "ones", [P, P])
            abs_sum = sbuf(st, "abs_sum", [P, 2])
            table_filler = sbuf(st, "table_filler", [P, 1])
            thr = sbuf(st, "thr", [P, 2])
            minus_thr = sbuf(st, "minus_thr", [P, 2])
            x_first = sems("x_first")
            x_second, x_rest = sem("x_second"), sem("x_rest")
            wa_loaded = [sem(f"wa_loaded_{part}") for part in ("q", "kv", "a")]
            w12_loaded, wvo_loaded = [sem("w1_loaded"), sem("w2_loaded")], sem("wvo_loaded")
            gamma_loaded, bias_loaded = sem("gamma_loaded"), sem("bias_loaded")
            ident_zero, ident_done, consts_done = sem("ident_zero"), sem("ident_done"), sem("consts_done")
            wa_transposed, wa_high, wa_low = sem("wa_transposed"), sem("wa_high"), sem("wa_low")
            abs_done, sum_done, thr_step, below_done, tern_done = sem("abs_done"), sem("sum_done"), sem("thr_step"), sem("below_done"), sem("tern_done")
            wt_ready, wt_done = sem("wt_ready"), sem("wt_done")
            wvo_high, wvo_low = sem("wvo_high"), sem("wvo_low")

            rms_std = sbuf(st, "rms_std", [P, B, CH])
            rms_norm = sbuf(st, "rms_norm", [P, B, CH])
            rms_factor = sbuf(st, "rms_factor", [P, B, CH])
            gate = sbuf(st, "gate", [P, B, DC, BLK])
            scan = sbuf(st, "scan", [P, B, DC, BLK])
            carry = sbuf(st, "carry", [P, B * DC])
            y = sbuf(st, "y", [P, B, DC, BLK])
            std_done, rms_step, factor_done = sems("A_std"), sems("A_rmsstep"), sems("A_factor")
            kv_ready, a_ready, q_ready = sems("A_kv"), sems("A_a"), sems("A_q")
            gate_done, scan_done, carry_done, y_done = sems("A_gate"), sems("A_scan"), sems("A_carry"), sems("A_y")
            y_transposed, x_added, carry_zero = sems("A_yt"), sems("A_xadd"), sem("A_zero")
            XB, KV, AB, QB, YB = (0, 1), (2, 3), 4, 5, (6, 7)
            WAB, SUMB = (2, 3, 4), 6
            WT = 2 * DC * FF // BLK
            flat = "p a b -> p (a b)"
            block = st.enter_context(nc.Block())

            def stage_loop(eng, step):
                for b in range(B):
                    step(b, 0, True, False)
                with eng.Fori(1, NBLK - 1) as i:
                    for b in range(B):
                        step(b, i, False, False)
                for b in range(B):
                    step(b, NBLK - 1, False, True)

            def former(b, i, first):
                if b:
                    return 0, i
                return None if first else (1, i - 1)

            @block.sync
            def _(sp):
                def load_x(b, i, blocks, loaded):
                    sp.dma_start(rows(b, i, 0, blocks * CH).rearrange("p (n d) -> p n d", d=D),
                                 x_view[b, :, i * CH:(i + blocks) * CH, :]).then_inc(loaded, 16)
                for b in range(B):
                    load_x(b, 0, 1, x_first[b])
                wa_view = wqkva_d.rearrange("(n p) d -> p n d", p=P)
                for n in range(len(WAB)):
                    sp.dma_start(wa_nat[:, n * DC:(n + 1) * DC, :], wa_view[:, n * DC:(n + 1) * DC, :]).then_inc(wa_loaded[n], 16)
                sp.dma_start(gamma_sb[:, :], gamma_d.rearrange("(n p) -> p n", p=P), allow_slow_non_contiguous=True).then_inc(gamma_loaded, 16)
                sp.dma_start(w1_nat[:, :, :], w1_d.rearrange("(n p) d -> p n d", p=P)).then_inc(w12_loaded[0], 16)
                sp.dma_start(w2_nat[:, :, :], w2_d.rearrange("(n p) d -> p n d", p=P)).then_inc(w12_loaded[1], 16)
                for b in range(B):
                    load_x(b, 1, 1, x_second)
                sp.dma_start(wv_raw[:, :, :], wv_d.rearrange("(k p) c -> p k c", p=P)).then_inc(wvo_loaded, 16)
                sp.dma_start(wo_raw[:, :].rearrange("p (n d) -> p n d", d=D),
                             wo_d.rearrange("(n p) d -> p n d", p=P)).then_inc(wvo_loaded, 16)
                for b in range(B):
                    load_x(b, 2, NBLK - 2, x_rest)
                sp.dma_start(b1_sb[:, :], b1_d.rearrange("(n p) -> p n", p=P), allow_slow_non_contiguous=True).then_inc(bias_loaded, 16)
                sp.dma_start(b2_sb[:, :], b2_d.partition_broadcast(P)).then_inc(bias_loaded, 16)

            @block.gpsimd
            def _(pool):
                start_counts(pool, ln.vare_done, ln.rstd_done, std_done)
                nc.gpsimd.memset(ident[:, :], 0.0).then_inc(ident_zero, 1)
                nc.gpsimd.memset(ones[:, :], 1.0).then_inc(consts_done, 1)
                nc.gpsimd.memset(minus_half[:, :], -0.5).then_inc(consts_done, 1)
                nc.gpsimd.memset(plus_half[:, :], 0.5).then_inc(consts_done, 1)
                nc.gpsimd.memset(ln_eps[:, :], LN_EPS).then_inc(consts_done, 1)
                pool.wait_ge(ident_zero, 1)
                nc.gpsimd.affine_select(out=ident[:, :], in_=ident[:, :], compare_op=ALU.not_equal, fill=1.0,
                                        base=0, pattern=[[-1, P]], channel_multiplier=1).then_inc(ident_done, 1)
                pool.wait_ge(consts_done, 4)

                def prepare(b, n):
                    ln.pool_rstd(pool, b, n)
                    nc.gpsimd.tensor_tensor(rms_std[:, b, :], ln_moments[:, b, :, 1], plus_half[:, :],
                                            ALU.pow).then_inc(std_done[b], 1)

                def find_below(n, nat):
                    if n:
                        pool.wait_ge(tern_done, n)
                    else:
                        pool.wait_ge(thr_step, 3)
                    nc.gpsimd.tensor_scalar(below[:, :], nat[:, :, :].rearrange(flat), minus_thr[:, n:n + 1], None,
                                            ALU.is_lt).then_inc(below_done, 1)

                def step(b, i, first, last):
                    if last:
                        ln.pool_rstd(pool, b, NBLK)
                        if b == 0:
                            find_below(1, w2_nat)
                            for n, (raw, hi, lo) in enumerate(((wv_raw[:, :, :], wv_hi[:, :, :], wv_lo[:, :, :]),
                                                               (wo_raw[:, :], wo_hi[:, :], wo_lo[:, :]))):
                                pool.wait_ge(wvo_high, n + 1)
                                nc.gpsimd.tensor_tensor(lo, raw, hi.bitcast(FP32), ALU.subtract).then_inc(wvo_low, 1)
                    else:
                        prepare(b, i + 1)
                    if first and b == 0:
                        find_below(0, w1_nat)
                for b in range(B):
                    prepare(b, 0)
                stage_loop(pool, step)

            @block.tensor
            def _(pe):
                start_counts(pe, ln.transposed, kv_ready, a_ready, q_ready, y_transposed)

                def transpose_wa():
                    for n in range(len(WAB)):
                        pe.wait_ge(wa_loaded[n], 16)
                        for k in range(DC):
                            for r in range(DC):
                                last = nc.tensor.transpose(bank[WAB[n]][:, k * D + r * P:k * D + (r + 1) * P],
                                                           wa_nat[:, n * DC + r, k * P:(k + 1) * P], ident[:, :])
                        last.then_inc(wa_transposed, 1)

                def transpose_ternary(g):
                    pe.wait_ge(tern_done, 1 if g < WT // 2 else 2)
                    if g < WT // 2:
                        pe.wait_ge(ln.low_done[1], START + NBLK * DC)
                    else:
                        pe.wait_ge(ln.low_done[0], START + (NBLK + 1) * DC)
                    if g > 1:
                        pe.wait_ge(wt_done, g - 1)
                    for m in range(4):
                        if g < WT // 2:
                            k, r = g // 2, (g % 2) * 4 + m
                            src = w1_nat[:, r, k * P:(k + 1) * P]
                        else:
                            f, k = 2 * (g - WT // 2) + m // 2, m % 2
                            src = w2_nat[:, k, f * P:(f + 1) * P]
                        last = nc.tensor.transpose(bank[XB[g % 2]][:, m * P:(m + 1) * P], src, ident[:, :])
                    last.then_inc(wt_ready, 1)

                def project(b, i, h):
                    if h == 0:
                        pe.wait_ge(ln.low_done[b], START + (i + 1) * DC)
                    other = 1 - b
                    for what, dst, part, ready in (("kv", KV[h], 1, kv_ready), ("a", AB, 2, a_ready), ("q", QB, 0, q_ready)):
                        if what == "kv":
                            pe.wait_ge(scan_done[other], START + (i + b) * DC - (DC - 1 - h if b else 0))
                        elif h:
                            pe.wait_ge((gate_done if what == "a" else y_done)[b], START + i * DC + 1)
                        else:
                            pe.wait_ge((gate_done if what == "a" else y_done)[other], START + (i + b) * DC)
                        for k in range(DC):
                            cols = slice(part * D + h * P, part * D + (h + 1) * P)
                            last = pe_split_product(bank[dst][:, :], wa_hi[:, k, cols], wa_lo[:, k, cols],
                                                    ln.xhi[:, b, k, :], ln.xlo[:, b, k, :], k, DC - 1)
                        last.then_inc(ready[b], 1)

                def transpose_y(b, i):
                    pe.wait_ge(x_added[1 - b], START + (i + b) * 2)
                    for h in range(DC):
                        pe.wait_ge(y_done[b], START + i * DC + h + 1)
                        for c in range(CH):
                            last = nc.tensor.transpose(bank[YB[c // 2]][:, (c % 2) * D + h * P:(c % 2) * D + (h + 1) * P],
                                                       y[:, b, h, c * P:(c + 1) * P], ident[:, :])
                    last.then_inc(y_transposed[b], 1)

                def prepare(b, n):
                    if b:
                        pe.wait_ge(ln.low_done[0], START + (n + 1) * DC)
                    else:
                        pe.wait_ge(ln.low_done[1], START + n * DC)
                    ln.pe_transpose(pe, b, n, XB)

                def step(b, i, first, last):
                    project(b, i, 0)
                    if last and b:
                        pe.wait_ge(wt_done, WT // 2)
                    prepare(1 - b, i + b)
                    if former(b, i, first):
                        transpose_y(*former(b, i, first))
                    project(b, i, 1)
                    if first and b == 0:
                        pe.wait_ge(abs_done, 2)
                        nc.tensor.matmul(bank[SUMB][:, 0:2], ones[:, :], abs_sum[:, :], start=True, stop=True)\
                            .then_inc(sum_done, 1)
                        pe.wait_ge(thr_step, 1)
                    if last:
                        for g in range(b * WT // B, (b + 1) * WT // B):
                            transpose_ternary(g)

                pe.wait_ge(consts_done, 4)
                pe.wait_ge(ident_done, 1)
                transpose_wa()
                prepare(0, 0)
                pe.wait_ge(wa_low, len(WAB))
                stage_loop(pe, step)
                transpose_y(1, NBLK - 1)
                pe.wait_ge(wt_done, WT)
                prepare(1, NBLK)

            @block.scalar
            def _(act):
                start_counts(act, ln.high_done, gate_done)
                def step(b, i, first, last):
                    for h in range(DC):
                        act.wait_ge(a_ready[b], START + i * DC + h + 1)
                        act.wait_ge(scan_done[b], START + i * DC)
                        nc.scalar.activation(gate[:, b, h, :], bank[AB][:, :], ACT.Sigmoid).then_inc(gate_done[b], 1)
                        if h == 0:
                            ln.act_high(act, 1 - b, i + b, XB, None if last and b else gamma_sb)
                    if last:
                        for g in range(b * WT // B, (b + 1) * WT // B):
                            act.wait_ge(wt_ready, g + 1)
                            dst = (w1t if g < WT // 2 else w2t)[:, :, :].rearrange(flat)
                            cols = slice(g % (WT // 2) * BLK, (g % (WT // 2) + 1) * BLK)
                            nc.scalar.copy(dst[:, cols], bank[XB[g % 2]][:, :]).then_inc(wt_done, 1)
                    if first:
                        act.wait_ge(wvo_loaded, 32)
                        if b == 0:
                            nc.scalar.copy(wv_hi[:, :, :], wv_raw[:, :, :]).then_inc(wvo_high, 1)
                        else:
                            nc.scalar.copy(wo_hi[:, :], wo_raw[:, :]).then_inc(wvo_high, 1)

                for n in range(len(WAB)):
                    act.wait_ge(wa_transposed, n + 1)
                    nc.scalar.copy(wa_hi[:, :, n * D:(n + 1) * D],
                                   bank[WAB[n]][:, :].rearrange("p (k d) -> p k d", k=DC)).then_inc(wa_high, 1)
                act.wait_ge(gamma_loaded, 16)
                ln.act_high(act, 0, 0, XB, gamma_sb)
                for n, (nat, unused) in enumerate(((w1_nat, below[:, :]), (w2_nat, scan[:, :, :, :].rearrange("p a b c -> p (a b c)")))):
                    act.wait_ge(w12_loaded[n], 16)
                    nc.scalar.activation(unused, nat[:, :, :].rearrange(flat), ACT.Abs,
                                         accum_out=abs_sum[:, n:n + 1]).then_inc(abs_done, 1)
                stage_loop(act, step)
                ln.act_high(act, 1, NBLK, XB)
                act.wait_ge(bias_loaded, 32)
                nc.scalar.activation(table_filler[:, :], b1_sb[:, 0:1], ACT.Gelu)

            @block.vector
            def _(dve):
                start_counts(dve, ln.stats_done, ln.moments_done, ln.normalised, ln.low_done, rms_step, factor_done,
                             scan_done, carry_done, y_done, x_added)

                def normalise(b, i):
                    dve.wait_ge(std_done[b], START + i + 1)
                    nc.vector.scalar_tensor_tensor(rms_norm[:, b, :], ln_rstd[:, b, :], float(D) ** 0.5, rms_std[:, b, :],
                                                   ALU.mult, ALU.mult).then_inc(rms_step[b], 1)
                    dve.wait_ge(rms_step[b], START + 3 * i + 1)
                    nc.vector.tensor_scalar(rms_norm[:, b, :], rms_norm[:, b, :], RMS_EPS, None, ALU.max).then_inc(rms_step[b], 1)
                    dve.wait_ge(rms_step[b], START + 3 * i + 2)
                    nc.vector.reciprocal(rms_norm[:, b, :], rms_norm[:, b, :]).then_inc(rms_step[b], 1)
                    dve.wait_ge(rms_step[b], START + 3 * i + 3)
                    nc.vector.scalar_tensor_tensor(rms_factor[:, b, :], ln_rstd[:, b, :], float(D) ** 0.5, rms_norm[:, b, :],
                                                   ALU.mult, ALU.mult).then_inc(factor_done[b], 1)
                    dve.wait_ge(factor_done[b], START + i + 1)
                    ln.dve_normalise(dve, b, i, i, rms_factor)

                def scan_half(b, i, h):
                    dve.wait_ge(gate_done[b], START + i * DC + h + 1)
                    dve.wait_ge(kv_ready[b], START + i * DC + h + 1)
                    dve.wait_ge(carry_done[b], START + i * DC + h)
                    nc.vector.tensor_tensor_scan(scan[:, b, h, :], gate[:, b, h, :], bank[KV[h]][:, :],
                                                 carry[:, b * DC + h:b * DC + h + 1], ALU.mult, ALU.add)\
                        .then_inc(scan_done[b], 1)
                    dve.wait_ge(scan_done[b], START + i * DC + h + 1)
                    nc.vector.tensor_copy(carry[:, b * DC + h:b * DC + h + 1],
                                          scan[:, b, h, BLK - 1:BLK]).then_inc(carry_done[b], 1)
                    dve.wait_ge(q_ready[b], START + i * DC + h + 1)
                    if h == 0:
                        dve.wait_ge(y_transposed[b], START + i)
                    nc.vector.tensor_tensor(y[:, b, h, :], bank[QB][:, :], scan[:, b, h, :],
                                            ALU.mult).then_inc(y_done[b], 1)

                def add_block(b, i):
                    dve.wait_ge(y_transposed[b], START + i + 1)
                    for j in range(2):
                        nc.vector.tensor_tensor(rows(b, i, 2 * j, 2), bank[YB[j]][:, :], rows(b, i, 2 * j, 2),
                                                ALU.add).then_inc(x_added[b], 1)

                def set_thresholds():
                    dve.wait_ge(sum_done, 1)
                    nc.vector.tensor_scalar(thr[:, :], bank[SUMB][:, 0:2], 1.0 / (FF * D), 1e-8, ALU.mult, ALU.max).then_inc(thr_step, 1)
                    dve.wait_ge(thr_step, 1)
                    nc.vector.tensor_scalar(minus_thr[:, :], thr[:, :], -0.5, None, ALU.mult).then_inc(thr_step, 1)
                    dve.wait_ge(thr_step, 2)
                    nc.vector.tensor_scalar(thr[:, :], thr[:, :], 0.5, None, ALU.mult).then_inc(thr_step, 1)
                    dve.wait_ge(thr_step, 3)

                def make_ternary(n, nat):
                    w = nat[:, :, :].rearrange(flat)
                    dve.wait_ge(below_done, n + 1)
                    nc.vector.scalar_tensor_tensor(w, w, thr[:, n:n + 1], below[:, :], ALU.is_gt, ALU.subtract)\
                        .then_inc(tern_done, 1)

                def statistics(b, i, first, last):
                    if last:
                        dve.wait_ge(x_added[b], START + 2)
                        ln.dve_statistics(dve, b, 0, NBLK)
                    else:
                        dve.wait_ge(x_second if first else x_rest, 16 * B)
                        ln.dve_statistics(dve, b, i + 1, i + 1)

                def step(b, i, first, last):
                    if last and b:
                        dve.wait_ge(ln.rstd_done[0], START + NBLK + 1)
                        ln.dve_normalise(dve, 0, 0, NBLK, ln_rstd)
                    else:
                        normalise(1 - b, i + b)
                    statistics(b, i, first, last)
                    scan_half(b, i, 0)
                    ln.dve_low(dve, 1 - b, i + b, XB, None if last and b else gamma_sb)
                    if former(b, i, first):
                        add_block(*former(b, i, first))
                    scan_half(b, i, 1)
                    if first and b == 0:
                        set_thresholds()
                    if first and b:
                        make_ternary(0, w1_nat)
                    if last and b == 0:
                        make_ternary(1, w2_nat)

                nc.vector.memset(carry[:, :], 0.0).then_inc(carry_zero, 1)
                dve.wait_ge(carry_zero, 1)
                dve.wait_ge(x_first[0], 16)
                ln.dve_statistics(dve, 0, 0, 0)
                dve.wait_ge(x_first[1], 16)
                ln.dve_statistics(dve, 1, 0, 0)
                normalise(0, 0)
                for n in range(len(WAB)):
                    dve.wait_ge(wa_high, n + 1)
                    cols = slice(n * D, (n + 1) * D)
                    nc.vector.tensor_tensor(wa_lo[:, :, cols], bank[WAB[n]][:, :].rearrange("p (k d) -> p k d", k=DC),
                                            wa_hi[:, :, cols].bitcast(FP32), ALU.subtract).then_inc(wa_low, 1)
                dve.wait_ge(gamma_loaded, 16)
                ln.dve_low(dve, 0, 0, XB, gamma_sb)
                stage_loop(dve, step)
                dve.wait_ge(ln.rstd_done[1], START + NBLK + 1)
                ln.dve_normalise(dve, 1, 0, NBLK, ln_rstd)
                add_block(1, NBLK - 1)
                ln.dve_low(dve, 1, NBLK, XB)

        wqa.close()

        def feed_forward(tag, stage, w1t, w2t, final):
            with ExitStack() as st:
                sem, sems = semaphores(st)
                hidden = sbuf(st, f"{tag}_hidden", [P, 4, BLK])
                hid_hi = sbuf(st, f"{tag}_hid_hi", [P, B, FC, BLK], FP32R)
                hid_lo = sbuf(st, f"{tag}_hid_lo", [P, B, FC, BLK], FP32R)
                h_ready, gelu_done, hhigh_done, hlow_done = sem(f"{tag}_h"), sem(f"{tag}_gelu"), sem(f"{tag}_hhigh"), sem(f"{tag}_hlow")
                out_ready, x_added, b2_added = sems(f"{tag}_out"), sems(f"{tag}_xadd"), sems(f"{tag}_b2")
                stored, w_saved = sem(f"{tag}_store"), sem(f"{tag}_wsave")
                n0 = stage * NBLK
                XB, HB, OB = (0, 1), (2, 3), ((4, 5), (6, 7))
                LAG = 2
                block = st.enter_context(nc.Block())

                def steps(iteration, tail):
                    def run(eng):
                        iteration(0, True, False)
                        with eng.Fori(1, NBLK - 1) as i:
                            iteration(i, False, False)
                        iteration(NBLK - 1, False, True)
                        tail()
                    return run

                def to_prepare(b, i, first, last):
                    if b == 0:
                        return None if first else (1, i, n0 + i)
                    if last:
                        return None if final else (0, 0, n0 + NBLK)
                    return 0, i + 1, n0 + i + 1

                def former(b, i, first):
                    if b:
                        return 0, i
                    return None if first else (1, i - 1)

                @block.sync
                def _(sp):
                    if not final:
                        sp.dma_start(w1t_dram, w1t.rearrange("p a b -> p (a b)").bitcast(FP32)).then_inc(w_saved, 16)
                        sp.dma_start(w2t_dram, w2t.rearrange("p a b -> p (a b)").bitcast(FP32)).then_inc(w_saved, 16)
                        sp.wait_ge(w_saved, 32)
                    if final:
                        with sp.Fori(0, NBLK - 1) as i:
                            for b in range(B):
                                sp.wait_ge(x_added[b], START + (i + 1) * 2)
                                sp.dma_start(out_view[b, :, bass.ds(i * CH, CH), :],
                                             rows(b, i, 0, CH).rearrange("p (n d) -> p n d", d=D)).then_inc(stored, 16)
                        last = NBLK - 1
                        for b in range(B):
                            for j in range(2):
                                sp.wait_ge(x_added[b], START + last * 2 + j + 1)
                                sp.dma_start(out_view[b, :, last * CH + 2 * j:last * CH + 2 * j + 2, :],
                                             rows(b, last, 2 * j, 2).rearrange("p (n d) -> p n d", d=D)).then_inc(stored, 16)
                        sp.wait_ge(stored, 16 * B * (NBLK - 1) + 16 * B * 2)

                @block.gpsimd
                def _(pool):
                    start_counts(pool, b2_added)
                    def iteration(i, first, last):
                        for b in range(B):
                            if not (last and final):
                                ln.pool_rstd(pool, b, n0 + i + 1)
                            pool.wait_ge(ln.normalised[b], START + (n0 + i + 1) * CH)
                            nc.gpsimd.tensor_tensor(rows(b, i, 0, CH).rearrange("p (n d) -> p n d", d=D),
                                                    rows(b, i, 0, CH).rearrange("p (n d) -> p n d", d=D),
                                                    b2_sb[:, None, :].to_broadcast([P, CH, D]),
                                                    ALU.add).then_inc(b2_added[b], 1)
                    steps(iteration, lambda: None)(pool)

                @block.tensor
                def _(pe):
                    start_counts(pe, h_ready, out_ready)
                    def up(b, i, f, first):
                        n = b * FC + f
                        if f == 0:
                            pe.wait_ge(ln.low_done[b], START + (n0 + i + 1) * DC)
                        if not first or n > 1:
                            pe.wait_ge(gelu_done, START + i * (2 * FC) + n - 1)
                        for k in range(DC):
                            w = w1t[:, k, f * P:(f + 1) * P]
                            nc.tensor.matmul(bank[HB[f % 2]][:, :], w, ln.xhi[:, b, k, :], start=(k == 0), stop=False)
                            last = nc.tensor.matmul(bank[HB[f % 2]][:, :], w, ln.xlo[:, b, k, :],
                                                    start=False, stop=(k == DC - 1))
                        last.then_inc(h_ready, 1)

                    def down(b, i, part):
                        if part == 0:
                            pe.wait_ge(hlow_done, START + i * (2 * FC) + (b + 1) * FC)
                            pe.wait_ge(x_added[b], START + i * 2)
                        c = part // 2
                        dst = bank[OB[b][c // 2]][:, (c % 2) * D:(c % 2 + 1) * D]
                        for f in range(part % 2 * (FC // 2), (part % 2 + 1) * (FC // 2)):
                            nc.tensor.matmul(dst, hid_hi[:, b, f, c * P:(c + 1) * P], w2t[:, f, :],
                                             start=(f == 0), stop=False)
                            last = nc.tensor.matmul(dst, hid_lo[:, b, f, c * P:(c + 1) * P], w2t[:, f, :],
                                                    start=False, stop=(f == FC - 1))
                        if part % 4 == 3:
                            last.then_inc(out_ready[b], 1)

                    def prepare(b, n):
                        if b:
                            pe.wait_ge(ln.low_done[0], START + (n + 1) * DC)
                        else:
                            pe.wait_ge(ln.low_done[1], START + n * DC)
                        ln.pe_transpose(pe, b, n, XB)

                    def iteration(i, first, last):
                        for b in range(B):
                            target, before = to_prepare(b, i, first, last), former(b, i, first)
                            for f in range(FC):
                                up(b, i, f, first)
                                if before and f >= LAG:
                                    down(*before, f - LAG)
                                if target and f == 3:
                                    prepare(target[0], target[2])
                            for part in range(FC - LAG, FC if before else 0):
                                down(*before, part)

                    def tail():
                        if not final:
                            prepare(1, n0 + NBLK)
                        for part in range(8):
                            down(1, NBLK - 1, part)

                    steps(iteration, tail)(pe)

                @block.scalar
                def _(act):
                    start_counts(act, gelu_done, hhigh_done)
                    def high(b, i, f):
                        act.wait_ge(gelu_done, START + i * (2 * FC) + b * FC + f + 1)
                        nc.scalar.copy(hid_hi[:, b, f, :], hidden[:, f % 4, :]).then_inc(hhigh_done, 1)

                    def iteration(i, first, last):
                        for b in range(B):
                            target = to_prepare(b, i, first, last)
                            act.wait_ge(out_ready[b], START + i * 2)
                            for f in range(FC):
                                n = b * FC + f
                                act.wait_ge(h_ready, START + i * (2 * FC) + n + 1)
                                if not first or n > 3:
                                    act.wait_ge(hlow_done, START + i * (2 * FC) + n - 3)
                                nc.scalar.activation(hidden[:, f % 4, :], bank[HB[f % 2]][:, :], ACT.Gelu,
                                                     bias=b1_sb[:, f:f + 1]).then_inc(gelu_done, 1)
                                if f:
                                    high(b, i, f - 1)
                                if target and f == 4:
                                    ln.act_high(act, target[0], target[2], XB)
                            high(b, i, FC - 1)

                    def tail():
                        if not final:
                            ln.act_high(act, 1, n0 + NBLK, XB)

                    steps(iteration, tail)(act)

                @block.vector
                def _(dve):
                    start_counts(dve, hlow_done, x_added)
                    def add_rows(b, i, j):
                        if j == 0:
                            dve.wait_ge(b2_added[b], START + i + 1)
                        dve.wait_ge(out_ready[b], START + i * 2 + j + 1)
                        nc.vector.tensor_tensor(rows(b, i, 2 * j, 2), bank[OB[b][j]][:, :], rows(b, i, 2 * j, 2),
                                                ALU.add).then_inc(x_added[b], 1)

                    def iteration(i, first, last):
                        for b in range(B):
                            target, before = to_prepare(b, i, first, last), former(b, i, first)
                            if target:
                                tb, block_of_rows, n = target
                                dve.wait_ge(ln.rstd_done[tb], START + n + 1)
                                ln.dve_normalise(dve, tb, block_of_rows, n, ln_rstd)
                            dve.wait_ge(out_ready[b], START + i * 2)
                            for f in range(FC):
                                dve.wait_ge(hhigh_done, START + i * (2 * FC) + b * FC + f + 1)
                                nc.vector.tensor_tensor(hid_lo[:, b, f, :], hidden[:, f % 4, :],
                                                        hid_hi[:, b, f, :].bitcast(FP32), ALU.subtract).then_inc(hlow_done, 1)
                                if f == 1 and not (last and final):
                                    if last:
                                        dve.wait_ge(x_added[b], START + 2)
                                    ln.dve_statistics(dve, b, 0 if last else i + 1, n0 + i + 1)
                                if last and b and not final and f == 3:
                                    dve.wait_ge(ln.rstd_done[1], START + n0 + NBLK + 1)
                                    ln.dve_normalise(dve, 1, 0, n0 + NBLK, ln_rstd)
                                if target and f == 4:
                                    ln.dve_low(dve, tb, n, XB)
                                if before and f == 5:
                                    add_rows(*before, 0)
                            if before:
                                add_rows(*before, 1)

                    def tail():
                        if not final:
                            ln.dve_low(dve, 1, n0 + NBLK, XB)
                        for j in range(2):
                            add_rows(1, NBLK - 1, j)

                    steps(iteration, tail)(dve)

        feed_forward("B", 1, w1t[:, :, :], w2t[:, :, :], False)
        tern.close()

        with ExitStack() as st:
            sem, sems = semaphores(st)
            causal = sbuf(st, "causal", [P, CH, P])
            v_all = sbuf(st, "v_all", [P, B, CH, H * DK])
            w_raw = sbuf(st, "w_raw", [P, 2, DC, P])
            w_hi = sbuf(st, "w_hi", [P, 2, DC, P], FP32R)
            w_lo = sbuf(st, "w_lo", [P, 2, DC, P], FP32R)
            qt = sbuf(st, "qt", [P, B, BLK])
            kt = sbuf(st, "kt", [P, B, BLK])
            krow = sbuf(st, "krow", [P, B, CH, P])
            vrow = sbuf(st, "vrow", [P, B, CH, P])
            scores = sbuf(st, "scores", [P, B, 2, CH, P])
            ut = sbuf(st, "ut", [P, B, BLK])
            urow = sbuf(st, "urow", [P, B, CH, P])
            ot_hi = sbuf(st, "ot_hi", [P, B, BLK], FP32R)
            ot_lo = sbuf(st, "ot_lo", [P, B, BLK], FP32R)
            s_state = sbuf(st, "s_state", [P, B, CH + 1, P])
            p_state = sbuf(st, "p_state", [P, B, CH + 1, P])
            s_carry = sbuf(st, "s_carry", [P, B * PAIRS * P])
            p_carry = sbuf(st, "p_carry", [P, B * PAIRS * P])

            w_loaded, w_high, w_low = sem("C_wload"), sem("C_whigh"), sem("C_wlow")
            tern_loaded = sem("C_ternload")
            mask_zero, masks_done, carry_zero = sem("C_maskzero"), sem("C_masks"), sem("C_zero")
            v_ready, v_stored = sem("C_v"), sem("C_vstore")
            q_ready, k_ready, qt_done, kt_done = sems("C_q"), sems("C_k"), sems("C_qt"), sems("C_kt")
            krow_ready, krow_done = sems("C_krp"), sems("C_krow")
            a_ready, a_masked, b_ready, b_masked = sems("C_a"), sems("C_am"), sems("C_b"), sems("C_bm")
            s_ready, s_summed = sems("C_s"), sems("C_ss")
            p_ready, p_summed = sems("C_p"), sems("C_ps")
            ut_ready, ut_done, urow_ready, urow_done = sems("C_utp"), sems("C_ut"), sems("C_urp"), sems("C_urow")
            o_ready, o_high, o_low = sems("C_o"), sems("C_oh"), sems("C_ol")
            out_ready, x_added = sems("C_out"), sems("C_xadd")
            s_carried, p_carried, vrow_done = sems("C_sc"), sems("C_pc"), sems("C_vr")

            QB, KB, AB = (0, 2), (1, 3), ((0, 1), (2, 3))
            KRB, UB, URB, PB = (4, 5), (4, 5), (4, 5), (4, 5)
            SB, OB, YB = (6, 7), (6, 7), ((4, 5), (6, 7))
            XB = ((0, 1), (2, 3))
            VB = (4, 5, 6, 7)
            V_OUT = B * CH * 2
            n0 = 2 * NBLK
            block = st.enter_context(nc.Block())

            def unit_loops(eng, block_start, unit):
                def one_block(i, last):
                    block_start(i)
                    with eng.Fori(0, PAIRS - 1) as p:
                        unit(i, p, i * PAIRS + p, False, False)
                    unit(i, PAIRS - 1, i * PAIRS + (PAIRS - 1), True, last)
                with eng.Fori(0, NBLK - 1) as i:
                    one_block(i, False)
                one_block(NBLK - 1, True)

            @block.sync
            def _(sp):
                start_counts(sp, w_loaded)
                with sp.Fori(0, NBLK) as i:
                    with sp.Fori(0, PAIRS) as p:
                        sp.wait_ge(w_low, START + i * PAIRS + p)
                        sp.dma_start(w_raw[:, 0:1, :, :],
                                     wq_view[:, bass.ds(p, 1)]).then_inc(w_loaded, 16)
                        sp.dma_start(w_raw[:, 1:2, :, :],
                                     wk_view[:, bass.ds(p, 1)]).then_inc(w_loaded, 16)
                sp.wait_ge(v_ready, START + NBLK * V_OUT)
                sp.dma_start(wv_hi[:, :, :].rearrange("p a b -> p (a b)").bitcast(FP32), w1t_dram).then_inc(tern_loaded, 16)
                sp.dma_start(wv_lo[:, :, :].rearrange("p a b -> p (a b)").bitcast(FP32), w2t_dram).then_inc(tern_loaded, 16)
                sp.wait_ge(tern_loaded, 32)

            @block.gpsimd
            def _(pool):
                start_counts(pool, v_ready, q_ready, k_ready, krow_ready, a_ready, b_ready,
                             s_ready, p_ready, ut_ready, urow_ready, o_ready, out_ready)
                nc.gpsimd.memset(causal[:, :, :], 1.0).then_inc(mask_zero, 1)
                pool.wait_ge(mask_zero, 1)
                nc.gpsimd.affine_select(out=causal[:, :, :], in_=causal[:, :, :], compare_op=ALU.is_ge, fill=0.0,
                                        base=0, pattern=[[0, CH], [1, P]], channel_multiplier=-1).then_inc(masks_done, 1)
                with pool.Fori(1, NBLK + 1) as i:
                    for b in range(B):
                        ln.pool_rstd(pool, b, n0 + i)

            @block.tensor
            def _(pe):
                def block_start(i):
                    for b in range(B):
                        pe.wait_ge(ln.low_done[b], START + (n0 + i + 1) * DC)
                        for c in range(CH):
                            for half in range(2):
                                n = (b * CH + c) * 2 + half
                                if n < len(VB):
                                    pe.wait_ge(x_added[n // 2], START + i * PAIRS * 2)
                                else:
                                    pe.wait_ge(v_stored, START + i * V_OUT + n - len(VB) + 1)
                                dst = bank[VB[n % len(VB)]][:, :]
                                for k in range(DC):
                                    x_hi, x_lo = ln.xhi[:, b, k, c * P:(c + 1) * P], ln.xlo[:, b, k, c * P:(c + 1) * P]
                                    cols = slice(half * BLK, (half + 1) * BLK)
                                    nc.tensor.matmul(dst, x_hi, wv_hi[:, k, cols], start=(k == 0), stop=False)
                                    nc.tensor.matmul(dst, x_hi, wv_lo[:, k, cols], start=False, stop=False)
                                    last = nc.tensor.matmul(dst, x_lo, wv_hi[:, k, cols], start=False, stop=(k == DC - 1))
                                last.then_inc(v_ready, 1)
                    for b in range(B):
                        project(b, i * PAIRS)

                def project(b, u):
                    pe.wait_ge(w_low, START + u + 1)
                    for part, dst, ready in ((0, QB[b], q_ready), (1, KB[b], k_ready)):
                        for k in range(DC):
                            last = pe_split_product(bank[dst][:, :], w_hi[:, part, k, :], w_lo[:, part, k, :],
                                                    ln.xhi[:, b, k, :], ln.xlo[:, b, k, :], k, DC - 1)
                        last.then_inc(ready[b], 1)

                def scores_of(keys, b, ready):
                    for c in range(CH):
                        tok = slice(c * P, (c + 1) * P)
                        for h in range(2):
                            hd = slice(h * DK, (h + 1) * DK)
                            last = nc.tensor.matmul(bank[AB[b][h]][:, tok], keys[hd, b, tok], qt[hd, b, tok], start=True, stop=True)
                            if c == CH - 1:
                                last.then_inc(ready[b], 1)

                def by_scores(row, dst, b):
                    for c in range(CH):
                        tok = slice(c * P, (c + 1) * P)
                        for h in range(2):
                            hd = slice(h * DK, (h + 1) * DK)
                            nc.tensor.matmul(bank[dst[b]][hd, tok], row[:, b, c, hd], scores[:, b, h, c, :],
                                             start=(c == 0), stop=False, skip_group_check=True)

                def by_state(pe, state, dst, b, u, summed):
                    for c in range(CH):
                        tok = slice(c * P, (c + 1) * P)
                        if c:
                            pe.wait_ge(summed[b], START + (u * CH + c) * 2)
                        last = nc.tensor.matmul(bank[dst[b]][:, tok], state[:, b, c, :], qt[:, b, tok],
                                                start=False, stop=(c == CH - 1), skip_group_check=True)
                    return last

                def unit(i, p, u, block_end, end):
                    pe.wait_ge(v_stored, START + (i + 1) * V_OUT)
                    for b in range(B):
                        pe.wait_ge(kt_done[b], START + u + 1)
                        pe.wait_ge(x_added[0], START + u * 2)
                        for c in range(CH):
                            tok = slice(c * P, (c + 1) * P)
                            last = nc.tensor.transpose(bank[KRB[b]][:, tok], kt[:, b, tok], ident[:, :])
                        last.then_inc(krow_ready[b], 1)
                    for b in range(B):
                        pe.wait_ge(qt_done[b], START + u + 1)
                        scores_of(kt, b, a_ready)
                        pe.wait_ge(krow_done[b], START + u + 1)
                        pe.wait_ge(x_added[1], START + u * 2)
                        for c in range(CH):
                            for h in range(2):
                                hd = slice(h * DK, (h + 1) * DK)
                                last = nc.tensor.matmul(bank[SB[b]][hd, c * DK:(c + 1) * DK], krow[:, b, c, hd], krow[:, b, c, hd],
                                                        start=True, stop=True)
                        last.then_inc(s_ready[b], 1)
                    for b in range(B):
                        pe.wait_ge(a_masked[b], START + (u + 1) * 2)
                        by_scores(krow, UB, b)
                        pe.wait_ge(s_carried[b], START + u + 1)
                        by_state(pe, s_state, UB, b, u, s_summed).then_inc(ut_ready[b], 1)
                    for b in range(B):
                        pe.wait_ge(ut_done[b], START + u + 1)
                        scores_of(ut, b, b_ready)
                    for b in range(B):
                        for c in range(CH):
                            tok = slice(c * P, (c + 1) * P)
                            last = nc.tensor.transpose(bank[URB[b]][:, tok], ut[:, b, tok], ident[:, :])
                        last.then_inc(urow_ready[b], 1)
                    for b in range(B):
                        pe.wait_ge(b_masked[b], START + (u + 1) * 2)
                        pe.wait_ge(vrow_done[b], START + u + 1)
                        pe.wait_ge(s_summed[b], START + (u + 1) * CH * 2)
                        by_scores(vrow, OB, b)
                        pe.wait_ge(urow_done[b], START + u + 1)
                        for c in range(CH):
                            for h in range(2):
                                hd = slice(h * DK, (h + 1) * DK)
                                last = nc.tensor.matmul(bank[PB[b]][hd, c * DK:(c + 1) * DK], urow[:, b, c, hd], vrow[:, b, c, hd],
                                                        start=True, stop=True)
                        last.then_inc(p_ready[b], 1)
                    for b in range(B):
                        pe.wait_ge(p_carried[b], START + u + 1)
                        by_state(pe, p_state, OB, b, u, p_summed).then_inc(o_ready[b], 1)
                        if block_end:
                            ln.pe_transpose(pe, b, n0 + i + 1, XB[b])
                        else:
                            project(b, u + 1)
                    for b in range(B):
                        pe.wait_ge(o_low[b], START + u + 1)
                        if b:
                            pe.wait_ge(o_low[0], START + u + 1)
                        else:
                            pe.wait_ge(p_summed[1], START + (u + 1) * CH * 2)
                        for c in range(CH):
                            tok = slice(c * P, (c + 1) * P)
                            dst = bank[YB[b][c // 2]][:, (c % 2) * D:(c % 2 + 1) * D]
                            w = [x[:, bass.ds(p * D, D)] for x in (wo_hi, wo_lo)]
                            nc.tensor.matmul(dst, ot_hi[:, b, tok], w[0], start=True, stop=False)
                            nc.tensor.matmul(dst, ot_hi[:, b, tok], w[1], start=False, stop=False)
                            last = nc.tensor.matmul(dst, ot_lo[:, b, tok], w[0], start=False, stop=True)
                            if c % 2:
                                last.then_inc(out_ready[b], 1)

                unit_loops(pe, block_start, unit)

            @block.scalar
            def _(act):
                start_counts(act, w_high, v_stored, qt_done, kt_done, krow_done, ut_done,
                             urow_done, o_high)
                def split_weights(u):
                    act.wait_ge(w_loaded, START + (u + 1) * 32)
                    act.wait_ge(k_ready[1], START + u)
                    nc.scalar.copy(w_hi[:, :, :, :], w_raw[:, :, :, :]).then_inc(w_high, 1)

                def block_start(i):
                    act.wait_ge(vrow_done[1], START + i * PAIRS)
                    for n in range(V_OUT):
                        act.wait_ge(v_ready, START + i * V_OUT + n + 1)
                        b, c, half = n // (2 * CH), n // 2 % CH, n % 2
                        nc.scalar.copy(v_all[:, b, c, half * BLK:(half + 1) * BLK], bank[VB[n % len(VB)]][:, :])\
                            .then_inc(v_stored, 1)

                    for b in range(B):
                        store_qk(b, i * PAIRS)

                def store_qk(b, u):
                    act.wait_ge(q_ready[b], START + u + 1)
                    act.wait_ge(o_ready[b], START + u)
                    nc.scalar.copy(qt[:, b, :], bank[QB[b]][:, :]).then_inc(qt_done[b], 1)
                    act.wait_ge(k_ready[b], START + u + 1)
                    act.wait_ge(a_ready[b], START + u * 2)
                    nc.scalar.copy(kt[:, b, :], bank[KB[b]][:, :]).then_inc(kt_done[b], 1)

                def unit(i, p, u, block_end, end):
                    for b in range(B):
                        act.wait_ge(krow_ready[b], START + u + 1)
                        act.wait_ge(ut_ready[b], START + u)
                        nc.scalar.copy(krow[:, b, :, :].rearrange("p c d -> p (c d)"), bank[KRB[b]][:, :]).then_inc(krow_done[b], 1)
                    if not end:
                        split_weights(u + 1)
                    for b in range(B):
                        act.wait_ge(ut_ready[b], START + u + 1)
                        nc.scalar.copy(ut[:, b, :], bank[UB[b]][:, :]).then_inc(ut_done[b], 1)
                    for b in range(B):
                        act.wait_ge(urow_ready[b], START + u + 1)
                        act.wait_ge(p_ready[b], START + u)
                        nc.scalar.copy(urow[:, b, :, :].rearrange("p c d -> p (c d)"), bank[URB[b]][:, :]).then_inc(urow_done[b], 1)
                    for b in range(B):
                        act.wait_ge(o_ready[b], START + u + 1)
                        act.wait_ge(out_ready[b], START + u * 2)
                        nc.scalar.copy(ot_hi[:, b, :], bank[OB[b]][:, :]).then_inc(o_high[b], 1)
                        if not block_end:
                            store_qk(b, u + 1)
                    if block_end:
                        for b in range(B):
                            ln.act_high(act, b, n0 + i + 1, XB[b])

                split_weights(0)
                unit_loops(act, block_start, unit)

            @block.vector
            def _(dve):
                start_counts(dve, x_added, w_low, a_masked, b_masked,
                             s_summed, s_carried, p_summed, p_carried, vrow_done, o_low)
                def split_weights(u):
                    dve.wait_ge(w_high, START + u + 1)
                    nc.vector.tensor_tensor(w_lo[:, :, :, :], w_raw[:, :, :, :], w_hi[:, :, :, :].bitcast(FP32),
                                            ALU.subtract).then_inc(w_low, 1)

                def mask_scores(b, u, ready, masked):
                    for h in range(2):
                        dve.wait_ge(ready[b], START + u * 2 + h + 1)
                        nc.vector.tensor_tensor(scores[:, b, h, :, :], bank[AB[b][h]][:, :].rearrange("p (c d) -> p c d", c=CH),
                                                causal[:, :, :], ALU.mult).then_inc(masked[b], 1)

                def sum_states(b, p, u, SBANK, state, carry, ready, summed, carried):
                    dve.wait_ge(ready[b], START + u + 1)
                    dve.wait_ge(carried[b], START + u + 1)
                    for c in range(CH):
                        if c:
                            dve.wait_ge(summed[b], START + (u * CH + c) * 2)
                        for h in range(2):
                            hd = slice(h * DK, (h + 1) * DK)
                            dst = state[hd, b, c + 1, hd] if c < CH - 1 else carry[hd, bass.ds((p + b * PAIRS) * P + h * DK, DK)]
                            nc.vector.tensor_tensor(dst, bank[SBANK[b]][hd, c * DK:(c + 1) * DK], state[hd, b, c, hd],
                                                    ALU.add).then_inc(summed[b], 1)

                def block_start(i):
                    pass

                def unit(i, p, u, block_end, end):
                    for b in range(B):
                        dve.wait_ge(s_summed[b], START + u * CH * 2)
                        dve.wait_ge(ut_ready[b], START + u)
                        nc.vector.tensor_copy(s_state[:, b, 0, :], s_carry[:, bass.ds((p + b * PAIRS) * P, P)])\
                            .then_inc(s_carried[b], 1)
                        dve.wait_ge(p_summed[b], START + u * CH * 2)
                        dve.wait_ge(o_ready[b], START + u)
                        nc.vector.tensor_copy(p_state[:, b, 0, :], p_carry[:, bass.ds((p + b * PAIRS) * P, P)])\
                            .then_inc(p_carried[b], 1)
                        dve.wait_ge(v_stored, START + (i + 1) * V_OUT)
                        nc.vector.tensor_copy(vrow[:, b, :, :], v_all[:, b, :, bass.ds(p * P, P)]).then_inc(vrow_done[b], 1)
                    for b in range(B):
                        mask_scores(b, u, a_ready, a_masked)
                        sum_states(b, p, u, SB, s_state, s_carry, s_ready, s_summed, s_carried)
                    if not end:
                        split_weights(u + 1)
                    after = 0 if end else i + 1
                    if block_end:
                        for b in range(B):
                            if end:
                                dve.wait_ge(x_added[b], START + PAIRS * 2)
                            ln.dve_statistics(dve, b, after, n0 + i + 1)
                    for b in range(B):
                        dve.wait_ge(ut_ready[b], START + u + 1)
                        mask_scores(b, u, b_ready, b_masked)
                    if block_end:
                        for b in range(B):
                            dve.wait_ge(ln.rstd_done[b], START + n0 + i + 2)
                            ln.dve_normalise(dve, b, after, n0 + i + 1, ln_rstd)
                    for b in range(B):
                        sum_states(b, p, u, PB, p_state, p_carry, p_ready, p_summed, p_carried)
                    for b in range(B):
                        dve.wait_ge(o_high[b], START + u + 1)
                        nc.vector.tensor_tensor(ot_lo[:, b, :], bank[OB[b]][:, :], ot_hi[:, b, :].bitcast(FP32),
                                                ALU.subtract).then_inc(o_low[b], 1)
                    for b in range(B):
                        if block_end:
                            ln.dve_low(dve, b, n0 + i + 1, XB[b])
                        for j in range(2):
                            dve.wait_ge(out_ready[b], START + u * 2 + j + 1)
                            nc.vector.tensor_tensor(rows(b, i, 2 * j, 2), bank[YB[b][j]][:, :], rows(b, i, 2 * j, 2),
                                                    ALU.add).then_inc(x_added[b], 1)

                nc.vector.memset(s_carry[:, :], 0.0).then_inc(carry_zero, 1)
                nc.vector.memset(p_carry[:, :], 0.0).then_inc(carry_zero, 1)
                nc.vector.memset(s_state[:, :, :, :], 0.0).then_inc(carry_zero, 1)
                nc.vector.memset(p_state[:, :, :, :], 0.0).then_inc(carry_zero, 1)
                split_weights(0)
                dve.wait_ge(carry_zero, 4)
                dve.wait_ge(masks_done, 1)
                unit_loops(dve, block_start, unit)

        feed_forward("D", 3, w1t_again, w2t_again, True)


_INS = ["L0_attn_a_x", "L0_attn_a_gamma", "L0_attn_a_w_qkva", "L0_attn_b_W_q", "L0_attn_b_W_k", "L0_attn_b_W_v",
        "L0_attn_b_W_o", "L0_ffn_W1", "L0_ffn_b1", "L0_ffn_W2", "L0_ffn_b2"]
_OUTS = [((B, T, D), "float32")]


def kernel(**inputs):
    import numpy as _np
    import concourse.bacc as _bacc
    from concourse import mybir as _mybir
    from concourse.bass_utils import run_bass_kernel_spmd as _run

    nc = _bacc.Bacc("TRN2", target_bir_lowering=False, num_devices=1)
    arrays, args = {}, []
    for name in _INS:
        a = _np.ascontiguousarray(inputs[name])
        arrays[f"in_{name}_dram"] = a
        args.append(nc.dram_tensor(f"in_{name}_dram", a.shape, _mybir.dt.from_np(a.dtype), kind="ExternalInput").ap())
    for i, (shape, dtype) in enumerate(_OUTS):
        dt = _mybir.dt.from_np(_np.dtype(dtype))
        args.append(nc.dram_tensor(f"out_{i}_dram", shape, dt, kind="ExternalOutput").ap())
    hybrid_kernel(nc, *args)
    r = _run(nc, [arrays], core_ids=[0])
    got = tuple(r.results[0][f"out_{i}_dram"] for i in range(len(_OUTS)))
    return got[0]
```
